# Optimizing a Trainium2 kernel written in Bass

```python
import numpy as np
import jax
import jax.numpy as jnp

def _softmax(x, axis=-1):
    return jax.nn.softmax(x, axis=axis)

def _gelu(x):
    return jax.nn.gelu(x, approximate=True)

def _silu(x):
    return jax.nn.silu(x)

def _sigmoid(x):
    return jax.nn.sigmoid(x)

def _layernorm(x, axis=-1, eps=1e-05):
    m = jnp.mean(x, axis=axis, keepdims=True)
    v = jnp.var(x, axis=axis, keepdims=True)
    return (x - m) / jnp.sqrt(v + eps)

def _scatter_add(tgt, idx, src, axis=0):
    return tgt.at[idx].add(src)

def _segment_sum(src, seg, n):
    return jax.ops.segment_sum(src, seg, n)
kernel_name = 'mk_seq_postln_d1_jaxref_r4_3ed2c7'

def setup_inputs(seed: int=0):
    np.random.seed(seed)
    _w = jnp.asarray

    def _L0_attn_setup():
        import jax, jax.numpy as jnp
        import numpy as np
        N_EMBD = 512
        N_HEADS = 16
        HEAD_DIM = N_EMBD // N_HEADS
        THETA = 10000.0

        def _rope_tables(seq_len, head_dim):
            inv = 1.0 / THETA ** (jnp.arange(0, head_dim, 2, dtype=jnp.float32) / head_dim)
            pos = jnp.arange(seq_len, dtype=jnp.float32)
            freqs = jnp.outer(pos, inv)
            return (jnp.cos(freqs)[None, :, None, :], jnp.sin(freqs)[None, :, None, :])

        def _apply_rope(t, cos, sin):
            B, S, H, D = t.shape
            tr = t.reshape(B, S, H, D // 2, 2)
            x0, x1 = (tr[..., 0], tr[..., 1])
            r0 = x0 * cos - x1 * sin
            r1 = x0 * sin + x1 * cos
            return jnp.stack([r0, r1], axis=-1).reshape(B, S, H, D)
        key = jax.random.key(seed)
        ks = jax.random.split(key, 9)
        B, S, E = (4, 512, N_EMBD)
        scale = 1.0 / np.sqrt(E)
        inp = {'x': jax.random.normal(ks[0], (B, S, E), dtype=jnp.float32), 'Wq': jax.random.normal(ks[1], (E, E), dtype=jnp.float32) * scale, 'bq': jnp.zeros((E,), dtype=jnp.float32), 'Wk': jax.random.normal(ks[2], (E, E), dtype=jnp.float32) * scale, 'bk': jnp.zeros((E,), dtype=jnp.float32), 'Wv': jax.random.normal(ks[3], (E, E), dtype=jnp.float32) * scale, 'bv': jnp.zeros((E,), dtype=jnp.float32), 'Wo': jax.random.normal(ks[4], (E, E), dtype=jnp.float32) * scale, 'bo': jnp.zeros((E,), dtype=jnp.float32)}
        return inp
    _L0_attn_in = _L0_attn_setup()

    def _L0_ffn_setup():
        import jax, jax.numpy as jnp
        import numpy as np
        HIDDEN = 512
        INTER = 1408
        B, S = (2, 512)

        def _ternary(key, shape):
            return jax.random.randint(key, shape, -1, 2).astype(jnp.float32)
        key = jax.random.key(seed)
        ks = jax.random.split(key, 7)
        x = jax.random.normal(ks[0], (B, S, HIDDEN), dtype=jnp.float32)
        gate_w = _ternary(ks[1], (INTER, HIDDEN))
        up_w = _ternary(ks[2], (INTER, HIDDEN))
        down_w = _ternary(ks[3], (HIDDEN, INTER))
        gate_s = jax.random.uniform(ks[4], (INTER,), minval=0.01, maxval=0.1, dtype=jnp.float32)
        up_s = jax.random.uniform(ks[5], (INTER,), minval=0.01, maxval=0.1, dtype=jnp.float32)
        down_s = jax.random.uniform(ks[6], (HIDDEN,), minval=0.01, maxval=0.1, dtype=jnp.float32)
        return {'x': x, 'gate_w': gate_w, 'up_w': up_w, 'down_w': down_w, 'gate_s': gate_s, 'up_s': up_s, 'down_s': down_s}
    _L0_ffn_in = _L0_ffn_setup()
    _d = {'L0_attn_x': _L0_attn_in['x'], 'L0_attn_Wq': _L0_attn_in['Wq'], 'L0_attn_bq': _L0_attn_in['bq'], 'L0_attn_Wk': _L0_attn_in['Wk'], 'L0_attn_bk': _L0_attn_in['bk'], 'L0_attn_Wv': _L0_attn_in['Wv'], 'L0_attn_bv': _L0_attn_in['bv'], 'L0_attn_Wo': _L0_attn_in['Wo'], 'L0_attn_bo': _L0_attn_in['bo'], 'L0_ffn_gate_w': _L0_ffn_in['gate_w'], 'L0_ffn_up_w': _L0_ffn_in['up_w'], 'L0_ffn_down_w': _L0_ffn_in['down_w'], 'L0_ffn_gate_s': _L0_ffn_in['gate_s'], 'L0_ffn_up_s': _L0_ffn_in['up_s'], 'L0_ffn_down_s': _L0_ffn_in['down_s']}
    _x0 = _d['L0_attn_x']
    _d['L0_attn_x'] = jax.random.normal(jax.random.fold_in(jax.random.key(seed), 1), (8, 1024, 512), dtype=_x0.dtype)
    del _x0
    return _d

def reference(L0_attn_x, L0_attn_Wq, L0_attn_bq, L0_attn_Wk, L0_attn_bk, L0_attn_Wv, L0_attn_bv, L0_attn_Wo, L0_attn_bo, L0_ffn_gate_w, L0_ffn_up_w, L0_ffn_down_w, L0_ffn_gate_s, L0_ffn_up_s, L0_ffn_down_s):

    def _L0_attn_ref(x, Wq, bq, Wk, bk, Wv, bv, Wo, bo):
        import jax, jax.numpy as jnp
        import numpy as np
        N_EMBD = 512
        N_HEADS = 16
        HEAD_DIM = N_EMBD // N_HEADS
        THETA = 10000.0

        def _rope_tables(seq_len, head_dim):
            inv = 1.0 / THETA ** (jnp.arange(0, head_dim, 2, dtype=jnp.float32) / head_dim)
            pos = jnp.arange(seq_len, dtype=jnp.float32)
            freqs = jnp.outer(pos, inv)
            return (jnp.cos(freqs)[None, :, None, :], jnp.sin(freqs)[None, :, None, :])

        def _apply_rope(t, cos, sin):
            B, S, H, D = t.shape
            tr = t.reshape(B, S, H, D // 2, 2)
            x0, x1 = (tr[..., 0], tr[..., 1])
            r0 = x0 * cos - x1 * sin
            r1 = x0 * sin + x1 * cos
            return jnp.stack([r0, r1], axis=-1).reshape(B, S, H, D)
        B, S, E = x.shape
        H, D = (N_HEADS, HEAD_DIM)
        q = (x @ Wq.T + bq).reshape(B, S, H, D)
        k = (x @ Wk.T + bk).reshape(B, S, H, D)
        v = (x @ Wv.T + bv).reshape(B, S, H, D)
        cos, sin = _rope_tables(S, D)
        q = _apply_rope(q, cos, sin)
        k = _apply_rope(k, cos, sin)
        qk = jnp.einsum('bshd,bstd->bsht', q, k) / jnp.sqrt(jnp.float32(D))
        att = jax.nn.softmax(qk, axis=-1)
        out = jnp.einsum('bsht,bstd->bshd', att, v)
        out = jnp.swapaxes(out, 1, 2).reshape(B, S, E)
        return out @ Wo.T + bo

    def _L0_ffn_ref(x, gate_w, up_w, down_w, gate_s, up_s, down_s):
        import jax, jax.numpy as jnp
        import numpy as np
        HIDDEN = 512
        INTER = 1408
        B, S = (2, 512)

        def _ternary(key, shape):
            return jax.random.randint(key, shape, -1, 2).astype(jnp.float32)
        b, s, h = x.shape
        xf = x.reshape(b * s, h)
        g = jnp.einsum('th,ih->ti', xf, gate_w) * gate_s
        u = jnp.einsum('th,ih->ti', xf, up_w) * up_s
        hdn = jax.nn.silu(g) * u
        out = jnp.einsum('ti,hi->th', hdn, down_w) * down_s
        return out.reshape(b, s, -1)
    x = L0_attn_x
    x = _layernorm(x + _L0_attn_ref(x, L0_attn_Wq, L0_attn_bq, L0_attn_Wk, L0_attn_bk, L0_attn_Wv, L0_attn_bv, L0_attn_Wo, L0_attn_bo), axis=-1)
    x = _layernorm(x + _L0_ffn_ref(x, L0_ffn_gate_w, L0_ffn_up_w, L0_ffn_down_w, L0_ffn_gate_s, L0_ffn_up_s, L0_ffn_down_s), axis=-1)
    return x

_drawn_inputs = setup_inputs


def setup_inputs(seed=0):
    import zlib

    import numpy as np

    out = dict(_drawn_inputs(seed))
    spreads = {'L0_attn_bq': (0.0, 0.1),
     'L0_attn_bk': (0.0, 0.1),
     'L0_attn_bv': (0.0, 0.1),
     'L0_attn_bo': (0.0, 0.1)}
    factors = {}
    for name, (base, spread) in spreads.items():
        noise = np.random.default_rng([zlib.crc32(name.encode()), seed]).standard_normal(out[name].shape)
        drawn = base * np.exp(spread * noise) if base else spread * noise
        out[name] = jnp.asarray(drawn.astype(out[name].dtype))
    for name, factor in factors.items():
        out[name] = (out[name] * factor).astype(out[name].dtype)
    return out
```

```python
from contextlib import ExitStack

import concourse.bass as bass
from concourse import mybir

ALU = mybir.AluOpType
ACT = mybir.ActivationFunctionType
AX = mybir.AxisListType
F32 = mybir.dt.float32
F32R = mybir.dt.float32r

P = 128
E = 512
H = 16
D = E // H
KE = E // P
C = 4
B4 = 4
A8 = 8
I = B4 * A8
INTER = 1408
NJ = INTER // P
CHUNK = 2 * KE * P + E
FFN = NJ * CHUNK
EPS = 1e-5
SCALE = float(D) ** -0.5


def at_least(eng, sem, count):
    if isinstance(count, int) and count <= 0:
        return
    eng.wait_ge(sem, count)


def steps(eng, step, peel, total, tail):
    for n in range(peel):
        step(n // 2, n % 2)
    with eng.Fori(peel // 2, total // 2) as i:
        for u in range(2):
            step(i, u)
    for n in range(total, total + tail):
        step(n // 2, n % 2)


def tile_of(i, u, lag, count):
    m, half, par = 2 * i + (u - lag), i + (u - lag) // 2, (u - lag) % 2
    if isinstance(m, int) and not 0 <= m < count:
        return None
    return m, half, par


def attention_phase(nc, x_cols, x_rows, rope, w_qkvo, biases, ffn_w, eye, head_mask, x1, ffn_hi, ffn_lo,
                    inexact):
    TILES = x_cols.shape[0]
    LAGS = 8
    SLABS = TILES // 2
    SLAB = FFN // SLABS
    assert SLAB * SLABS == FFN
    with ExitStack() as ctx:
        def sb(name, shape, dt=F32):
            return ctx.enter_context(nc.sbuf_tensor(name, shape, dt))

        def bank(name):
            return ctx.enter_context(nc.psum_tensor(name, [P, E], F32))

        def sem(name):
            return ctx.enter_context(nc.semaphore(name))

        w_raw = sb("w_raw", [P, 2, KE, E])
        w_hi = sb("w_hi", [P, 4, KE, E], F32R)
        w_lo = sb("w_lo", [P, 4, KE, E], F32R)
        bias = sb("bias", [P, 4, E])
        ident = sb("ident", [P, P])
        own_token = sb("own_token", [P, A8])
        xc = sb("xc", [P, 2, KE, P])
        xc_hi = sb("xc_hi", [P, 2, KE, P], F32R)
        xc_lo = sb("xc_lo", [P, 2, KE, P], F32R)
        rot = sb("rot", [P, 2, 2, D])
        qk_in = sb("qk_in", [P, 2, E])
        qk_cos = sb("qk_cos", [P, 2, E])
        qk_sin = sb("qk_sin", [P, 2, E])
        qk_rot = sb("qk_rot", [P, 2, E])
        v_in = sb("v_in", [P, E])
        qT = sb("qT", [P, 2, I, H])
        kX = sb("kX", [P, 2, I, C, H])
        vT = sb("vT", [P, 2, B4, H, A8])
        v8 = sb("v8", [P, 2, B4, P])
        prob = sb("prob", [P, 2, A8 * C, H])
        top = sb("top", [P, A8 * C])
        total = sb("total", [P, A8 * C])
        over = sb("over", [P, A8 * C])
        probN = sb("probN", [P, C, H, A8])
        probX = sb("probX", [P, C * B4, H, A8])
        aT_hi = sb("aT_hi", [P, 2, B4, P], F32R)
        aT_lo = sb("aT_lo", [P, 2, B4, P], F32R)
        res = sb("res", [P, 2, E])
        res_bo = sb("res_bo", [P, 2, E])
        y = sb("y", [P, 2, E])
        stats = sb("stats", [P, 6])
        mean_var = sb("mean_var", [P, 2, 2])
        rstd = sb("rstd", [P, 2])
        power = sb("power", [P, 1])
        x1_out = sb("x1_out", [P, 2, E])
        f_raw = sb("f_raw", [P, SLAB])
        f_hi = sb("f_hi", [P, SLAB], F32R)
        f_lo = sb("f_lo", [P, SLAB], F32R)
        lo_top = sb("lo_top", [P, SLABS])
        lo_top1 = sb("lo_top1", [P, 2])

        ps_qkv = [bank("ps_q"), bank("ps_k"), bank("ps_v")]
        ps_s, ps_p, ps_vt, ps_a, ps_o = bank("ps_s"), bank("ps_p"), bank("ps_vt"), bank("ps_a"), bank("ps_o")

        w_loaded = [[sem(f"w_loaded{w}_{k}") for k in range(KE)] for w in range(4)]
        w_hi_done, w_lo_done = sem("w_hi_done"), sem("w_lo_done")
        const_loaded = sem("const_loaded")
        kX_zeroed, power_set, idle_cleared = sem("kX_zeroed"), sem("power_set"), sem("idle_cleared")
        xc_loaded = [sem(f"xc_loaded{u}") for u in range(2)]
        rot_loaded = [sem(f"rot_loaded{u}") for u in range(2)]
        res_loaded = [sem(f"res_loaded{u}") for u in range(2)]
        x1_stored = [sem(f"x1_stored{u}") for u in range(2)]
        f_loaded, f_hi_done, f_lo_done = sem("f_loaded"), sem("f_hi_done"), sem("f_lo_done")
        f_hi_stored, f_lo_stored = sem("f_hi_stored"), sem("f_lo_stored")
        xhi_done, xlo_done = sem("xhi_done"), sem("xlo_done")
        proj_done = [sem(f"proj_done_{w}") for w in "qkv"]
        biased = [sem(f"biased_{w}") for w in "qkv"]
        cos_done = [sem(f"cos_done_{w}") for w in "qk"]
        sin_done = [sem(f"sin_done_{w}") for w in "qk"]
        rotated = [sem(f"rotated_{w}") for w in "qk"]
        turned = [sem(f"turned_{w}") for w in "qkv"]
        scores_done, max_done, sub_done, exp_done = sem("scores_done"), sem("max_done"), sem("sub_done"), sem("exp_done")
        sum_done, over_done, prob_done = sem("sum_done"), sem("over_done"), sem("prob_done")
        probT_done, spread_done, vt_done, v8_done = sem("probT_done"), sem("spread_done"), sem("vt_done"), sem("v8_done")
        av_done, ahi_done, alo_done, o_done = sem("av_done"), sem("ahi_done"), sem("alo_done"), sem("o_done")
        res_added, y_done, stats_done, aggr_done = sem("res_added"), sem("y_done"), sem("stats_done"), sem("aggr_done")
        rstd_ready, x1_done = sem("rstd_ready"), sem("x1_done")
        lo_seen, lo_reduced, lo_joined, flag_set = sem("lo_seen"), sem("lo_reduced"), sem("lo_joined"), sem("flag_set")

        block = ctx.enter_context(nc.Block())

        @block.sync
        def _(sp):
            for w in range(4):
                for k in range(KE):
                    if w >= 2:
                        sp.wait_ge(w_hi_done, KE * (w - 2) + k + 1)
                        sp.wait_ge(w_lo_done, KE * (w - 2) + k + 1)
                    sp.dma_start(w_raw[:, w % 2, k], w_qkvo[w, :, k]).then_inc(w_loaded[w][k], 16)
                    if w == 0 and k == 0:
                        sp.dma_start(xc[:, 0], x_cols[0]).then_inc(xc_loaded[0], 16)
                if w == 1:
                    for k in range(4):
                        sp.dma_start(bias[:, k], biases[k:k + 1, :].to_broadcast([P, E])).then_inc(const_loaded, 16)
                    sp.dma_start(ident[:, :], eye).then_inc(const_loaded, 16)
                    sp.dma_start(own_token[:, :], head_mask).then_inc(const_loaded, 16)

            def step(i, u):
                if t := tile_of(i, u, 0, TILES):
                    n, half, par = t
                    if not (isinstance(n, int) and n == 0):
                        at_least(sp, xhi_done, n - 1)
                        at_least(sp, xlo_done, n - 1)
                        sp.dma_start(xc[:, par], x_cols[n]).then_inc(xc_loaded[par], 16)
                    at_least(sp, rotated[1], n - 1)
                    sp.dma_start(rot[:, par], rope[n % rope.shape[0]]).then_inc(rot_loaded[par], 16)
                if t := tile_of(i, u, 3, TILES):
                    n, half, par = t
                    at_least(sp, res_added, n - 1)
                    sp.dma_start(res[:, par], x_rows[n]).then_inc(res_loaded[par], 16)
                if u == 0 and (t := tile_of(i, u, 2, TILES)):
                    slab = t[1]
                    at_least(sp, f_hi_done, slab)
                    at_least(sp, f_lo_done, slab)
                    sp.dma_start(f_raw[:, :], ffn_w[slab]).then_inc(f_loaded, 16)
                if u == 0 and (t := tile_of(i, u, 4, TILES)):
                    slab = t[1]
                    sp.wait_ge(f_hi_done, slab + 1)
                    sp.dma_start(ffn_hi[slab], f_hi[:, :].bitcast(F32)).then_inc(f_hi_stored, 16)
                    sp.wait_ge(f_lo_done, slab + 1)
                    sp.dma_start(ffn_lo[slab], f_lo[:, :].bitcast(F32)).then_inc(f_lo_stored, 16)
                if t := tile_of(i, u, 7, TILES):
                    n, half, par = t
                    sp.wait_ge(x1_done, n + 1)
                    sp.dma_start(x1[n], x1_out[:, par]).then_inc(x1_stored[par], 16)

            steps(sp, step, LAGS, TILES, LAGS)
            for u in range(2):
                sp.wait_ge(x1_stored[u], 16 * (TILES // 2))
            sp.wait_ge(f_hi_stored, 16 * SLABS)
            sp.wait_ge(f_lo_stored, 16 * SLABS)

        @block.tensor
        def _(pe):
            def project(out, hi, lo, w, sem_done, first_use):
                for k in range(KE):
                    if first_use:
                        pe.wait_ge(w_hi_done, KE * w + k + 1)
                        pe.wait_ge(w_lo_done, KE * w + k + 1)
                    pe.matmul(out, hi[:, k], w_hi[:, w, k], start=(k == 0), stop=False)
                    pe.matmul(out, hi[:, k], w_lo[:, w, k], start=False, stop=False)
                    last = pe.matmul(out, lo[:, k], w_hi[:, w, k], start=False, stop=(k == KE - 1))
                last.then_inc(sem_done, 1)

            def step(i, u):
                if t := tile_of(i, u, 1, TILES):
                    n, half, par = t
                    pe.wait_ge(xhi_done, n + 1)
                    pe.wait_ge(xlo_done, n + 1)
                    for w in range(3):
                        at_least(pe, biased[w], n)
                        project(ps_qkv[w][:, :], xc_hi[:, par], xc_lo[:, par], w, proj_done[w],
                                isinstance(n, int) and n == 0)
                if t := tile_of(i, u, 3, TILES):
                    n, half, par = t
                    pe.wait_ge(prob_done, n + 1)
                    at_least(pe, spread_done, n)
                    for c in range(C):
                        last = pe.transpose(ps_p[:, c * P:(c + 1) * P],
                                            probN[:, c].rearrange("p t a -> p (t a)"), ident[:, :])
                    last.then_inc(probT_done, 1)
                if t := tile_of(i, u, 2, TILES):
                    n, half, par = t
                    if isinstance(n, int) and n == 0:
                        pe.wait_ge(const_loaded, 16 * 6)
                        pe.wait_ge(idle_cleared, 1)
                    pe.wait_ge(turned[0], n + 1)
                    pe.wait_ge(turned[1], n + 1)
                    at_least(pe, sub_done, n)
                    for a in range(A8):
                        for b in range(B4):
                            last = pe.matmul(ps_s[32 * b:32 * b + H, a * C * H:(a + 1) * C * H],
                                             qT[:, par, A8 * b + a],
                                             kX[:, par, A8 * b + a].rearrange("p c t -> p (c t)"),
                                             start=True, stop=True, skip_group_check=True)
                    last.then_inc(scores_done, 1)
                    pe.wait_ge(turned[2], n + 1)
                    at_least(pe, v8_done, n)
                    for b in range(B4):
                        last = pe.transpose(ps_vt[:, b * P:(b + 1) * P],
                                            vT[:, par, b].rearrange("p h a -> p (h a)"), ident[:, :])
                    last.then_inc(vt_done, 1)
                if t := tile_of(i, u, 4, TILES):
                    n, half, par = t
                    pe.wait_ge(ahi_done, n + 1)
                    pe.wait_ge(alo_done, n + 1)
                    at_least(pe, y_done, n)
                    project(ps_o[:, :], aT_hi[:, par], aT_lo[:, par], 3, o_done,
                            isinstance(n, int) and n == 0)
                if t := tile_of(i, u, 3, TILES):
                    n, half, par = t
                    pe.wait_ge(spread_done, n + 1)
                    pe.wait_ge(v8_done, n + 1)
                    at_least(pe, ahi_done, n)
                    at_least(pe, alo_done, n)
                    for b in range(B4):
                        for c in range(C):
                            last = pe.matmul(ps_a[32 * c:32 * c + 32, b * P:(b + 1) * P],
                                             v8[:, par, b, 32 * c:32 * c + 32],
                                             probX[:, c * B4 + b].rearrange("p h a -> p (h a)"),
                                             start=True, stop=True, skip_group_check=True)
                    last.then_inc(av_done, 1)

            steps(pe, step, LAGS, TILES, LAGS)

        @block.scalar
        def _(act):
            def split_x(n, half, par):
                act.wait_ge(xc_loaded[par], 16 * (half + 1))
                at_least(act, proj_done[2], n - 1)
                act.activation(xc_hi[:, par], xc[:, par], ACT.Copy).then_inc(xhi_done, 1)

            for w in range(4):
                for k in range(KE):
                    act.wait_ge(w_loaded[w][k], 16)
                    act.activation(w_hi[:, w, k], w_raw[:, w % 2, k], ACT.Copy).then_inc(w_hi_done, 1)
                    if w == 0 and k == 0:
                        split_x(0, 0, 0)
            act.wait_ge(const_loaded, 16 * 6)

            def step(i, u):
                if t := tile_of(i, u, 3, TILES):
                    n, half, par = t
                    act.wait_ge(sub_done, n + 1)
                    act.activation(prob[:, par], prob[:, par], ACT.Exp, scale=SCALE).then_inc(exp_done, 1)
                if t := tile_of(i, u, 4, TILES):
                    n, half, par = t
                    act.wait_ge(av_done, n + 1)
                    at_least(act, o_done, n - 1)
                    act.activation(aT_hi[:, par].rearrange("p b r -> p (b r)"), ps_a[:, :], ACT.Copy)\
                        .then_inc(ahi_done, 1)
                if t := tile_of(i, u, 0, TILES):
                    n, half, par = t
                    if not (isinstance(n, int) and n == 0):
                        split_x(n, half, par)
                if u == 0 and (t := tile_of(i, u, 2, TILES)):
                    slab = t[1]
                    act.wait_ge(f_loaded, 16 * (slab + 1))
                    at_least(act, f_hi_stored, 16 * slab)
                    at_least(act, f_lo_done, slab)
                    act.activation(f_hi[:, :], f_raw[:, :], ACT.Copy).then_inc(f_hi_done, 1)
                if t := tile_of(i, u, 3, TILES):
                    n, half, par = t
                    act.wait_ge(probT_done, n + 1)
                    at_least(act, av_done, n)
                    for a in range(A8):
                        last = act.activation(
                            probX[:, :, :, a],
                            ps_p[:, :].rearrange("p (cb used h) -> p cb used h", used=2, h=H)[:, :, 0],
                            ACT.Copy, scale=own_token[:, a:a + 1])
                    last.then_inc(spread_done, 1)
                if t := tile_of(i, u, 2, TILES):
                    n, half, par = t
                    act.wait_ge(vt_done, n + 1)
                    at_least(act, av_done, n - 1)
                    act.activation(v8[:, par].rearrange("p b r -> p (b r)"), ps_vt[:, :], ACT.Copy)\
                        .then_inc(v8_done, 1)

            steps(act, step, LAGS, TILES, LAGS)

        @block.gpsimd
        def _(pool):
            pool.wait_ge(xhi_done, 1)
            pool.tensor_tensor(xc_lo[:, 0], xc[:, 0], xc_hi[:, 0].bitcast(F32), ALU.subtract).then_inc(xlo_done, 1)
            pool.memset(kX[:, :, :, :, :], 0.0).then_inc(kX_zeroed, 1)
            pool.memset(power[:, :], -0.5).then_inc(power_set, 1)
            pool.wait_ge(power_set, 1)

            def step(i, u):
                if t := tile_of(i, u, 5, TILES):
                    n, half, par = t
                    pool.wait_ge(aggr_done, n + 1)
                    pool.tensor_tensor(rstd[:, par:par + 1], mean_var[:, par, 1:2], power[:, :], ALU.pow)\
                        .then_inc(rstd_ready, 1)
                if t := tile_of(i, u, 0, TILES):
                    n, half, par = t
                    if not (isinstance(n, int) and n == 0):
                        pool.wait_ge(xhi_done, n + 1)
                        pool.tensor_tensor(xc_lo[:, par], xc[:, par], xc_hi[:, par].bitcast(F32), ALU.subtract)\
                            .then_inc(xlo_done, 1)
                if t := tile_of(i, u, 4, TILES):
                    n, half, par = t
                    if isinstance(n, int) and n == 0:
                        pool.wait_ge(const_loaded, 16 * 6)
                    pool.wait_ge(res_loaded[par], 16 * (half + 1))
                    at_least(pool, y_done, n - 1)
                    pool.tensor_tensor(res_bo[:, par], res[:, par], bias[:, 3], ALU.add).then_inc(res_added, 1)
                if t := tile_of(i, u, 1, TILES):
                    n, half, par = t
                    pool.wait_ge(rot_loaded[par], 16 * (half + 1))
                    for w in range(2):
                        pool.wait_ge(biased[w], n + 1)
                        at_least(pool, rotated[w], n)
                        pool.tensor_tensor(qk_cos[:, w].rearrange("p (h d) -> p h d", h=H),
                                           qk_in[:, w].rearrange("p (h d) -> p h d", h=H),
                                           rot[:, par, 0].unsqueeze(1).to_broadcast([P, H, D]), ALU.mult)\
                            .then_inc(cos_done[w], 1)
                if u == 0 and (t := tile_of(i, u, 2, TILES)):
                    slab = t[1]
                    pool.wait_ge(f_hi_done, slab + 1)
                    at_least(pool, f_lo_stored, 16 * slab)
                    at_least(pool, lo_seen, slab)
                    pool.tensor_tensor(f_lo[:, :], f_raw[:, :], f_hi[:, :].bitcast(F32), ALU.subtract)\
                        .then_inc(f_lo_done, 1)

            steps(pool, step, LAGS, TILES, LAGS)
            pool.wait_ge(lo_reduced, 1)
            pool.partition_all_reduce(lo_top1[:, 1:2], lo_top1[:, 0:1], P, bass.bass_isa.ReduceOp.max)\
                .then_inc(lo_joined, 1)

        @block.vector
        def _(dve):
            for w in range(4):
                for k in range(KE):
                    dve.wait_ge(w_hi_done, KE * w + k + 1)
                    dve.tensor_tensor(w_lo[:, w, k], w_raw[:, w % 2, k], w_hi[:, w, k].bitcast(F32),
                                      ALU.subtract).then_inc(w_lo_done, 1)
            dve.wait_ge(const_loaded, 16 * 6)
            dve.wait_ge(kX_zeroed, 1)
            dve.memset(ps_s[:, :], 0.0).then_inc(idle_cleared, 1)

            def turn(w, n, par):
                if w == 0:
                    at_least(dve, scores_done, n - 1)
                    dve.wait_ge(rotated[0], n + 1)
                    last = dve.transpose(qT[:, par].rearrange("p i h -> p h i"),
                                         qk_rot[:, 0].rearrange("p (h d) -> p h d", h=H))
                elif w == 1:
                    dve.wait_ge(rotated[1], n + 1)
                    for c in range(C):
                        last = dve.transpose(kX[32 * c:32 * c + 32, par, :, c].rearrange("p i h -> p h i"),
                                             qk_rot[32 * c:32 * c + 32, 1].rearrange("p (h d) -> p h d", h=H))
                else:
                    at_least(dve, vt_done, n - 1)
                    dve.wait_ge(biased[2], n + 1)
                    last = dve.transpose(vT[:, par].rearrange("p b h a -> p h b a"),
                                         v_in[:, :].rearrange("p (h b a) -> p h b a", h=H, b=B4))
                last.then_inc(turned[w], 1)

            def step(i, u):
                if t := tile_of(i, u, 3, TILES):
                    n, half, par = t
                    scores = ps_s[:, :].rearrange("p (g t) -> p g t", t=H)
                    dve.wait_ge(scores_done, n + 1)
                    dve.tensor_reduce(top[:, :], scores, AX.X, ALU.max).then_inc(max_done, 1)
                    dve.wait_ge(max_done, n + 1)
                    dve.tensor_tensor(prob[:, par], scores, top[:, :].unsqueeze(2).to_broadcast([P, A8 * C, H]),
                                      ALU.subtract).then_inc(sub_done, 1)
                if t := tile_of(i, u, 5, TILES):
                    n, half, par = t
                    dve.wait_ge(o_done, n + 1)
                    dve.wait_ge(res_added, n + 1)
                    dve.tensor_tensor(y[:, par], ps_o[:, :], res_bo[:, par], ALU.add).then_inc(y_done, 1)
                    dve.wait_ge(y_done, n + 1)
                    dve.bn_stats(stats[:, :], y[:, par]).then_inc(stats_done, 1)
                if t := tile_of(i, u, 4, TILES):
                    n, half, par = t
                    dve.wait_ge(ahi_done, n + 1)
                    at_least(dve, stats_done, 2 * (n - 1) + 1)
                    dve.tensor_tensor(aT_lo[:, par].rearrange("p b r -> p (b r)"), ps_a[:, :],
                                      aT_hi[:, par].rearrange("p b r -> p (b r)").bitcast(F32), ALU.subtract)\
                       .then_inc(alo_done, 1)
                if t := tile_of(i, u, 5, TILES):
                    n, half, par = t
                    if isinstance(n, int):
                        dve.wait_ge(stats_done, 2 * n + 1)
                    dve.bn_aggr(mean_var[:, par], stats[:, :]).then_inc(stats_done, 1)
                    dve.wait_ge(stats_done, 2 * n + 2)
                    dve.tensor_scalar(mean_var[:, par, 1:2], mean_var[:, par, 1:2], EPS, None, ALU.add)\
                       .then_inc(aggr_done, 1)
                if t := tile_of(i, u, 3, TILES):
                    n, half, par = t
                    dve.wait_ge(exp_done, n + 1)
                    dve.tensor_reduce(total[:, :], prob[:, par], AX.X, ALU.add).then_inc(sum_done, 1)
                    dve.wait_ge(sum_done, n + 1)
                    dve.reciprocal(over[:, :], total[:, :]).then_inc(over_done, 1)
                    dve.wait_ge(over_done, n + 1)
                    at_least(dve, probT_done, n)
                    dve.tensor_tensor(probN[:, :].rearrange("p c t a -> p a c t"),
                                      prob[:, par].rearrange("p (a c) t -> p a c t", a=A8),
                                      over[:, :].rearrange("p (a c) -> p a c", a=A8).unsqueeze(3)
                                      .to_broadcast([P, A8, C, H]), ALU.mult).then_inc(prob_done, 1)
                if t := tile_of(i, u, 1, TILES):
                    n, half, par = t
                    dve.wait_ge(rot_loaded[par], 16 * (half + 1))
                    for w in range(2):
                        dve.wait_ge(proj_done[w], n + 1)
                        at_least(dve, rotated[w], n)
                        at_least(dve, cos_done[w], n)
                        dve.tensor_tensor(qk_in[:, w], ps_qkv[w][:, :], bias[:, w], ALU.add).then_inc(biased[w], 1)
                        dve.wait_ge(biased[w], n + 1)
                        pair = qk_in[:, w].rearrange("p (h k two) -> p h k two", h=H, two=2)
                        dve.tensor_tensor(qk_sin[:, w].rearrange("p (h k two) -> p h k two", h=H, two=2),
                                          pair[:, :, :, ::-1],
                                          rot[:, par, 1].rearrange("p (k two) -> p k two", two=2).unsqueeze(1)
                                          .to_broadcast([P, H, D // 2, 2]), ALU.mult).then_inc(sin_done[w], 1)
                    dve.wait_ge(proj_done[2], n + 1)
                    at_least(dve, turned[2], n)
                    dve.tensor_tensor(v_in[:, :], ps_qkv[2][:, :], bias[:, 2], ALU.add).then_inc(biased[2], 1)
                    for w in range(2):
                        dve.wait_ge(cos_done[w], n + 1)
                        dve.wait_ge(sin_done[w], n + 1)
                        at_least(dve, turned[w], n)
                        dve.tensor_tensor(qk_rot[:, w], qk_cos[:, w], qk_sin[:, w], ALU.add).then_inc(rotated[w], 1)
                        if w == 0:
                            turn(2, n, par)
                        turn(w, n, par)
                if u == 0 and (t := tile_of(i, u, 2, TILES)):
                    slab = t[1]
                    dve.wait_ge(f_lo_done, slab + 1)
                    dve.tensor_reduce(lo_top[:, bass.ds(slab, 1)], f_lo[:, :].bitcast(F32), AX.X, ALU.max,
                                      apply_absolute_value=True).then_inc(lo_seen, 1)
                if t := tile_of(i, u, 5, TILES):
                    n, half, par = t
                    dve.wait_ge(rstd_ready, n + 1)
                    at_least(dve, x1_stored[par], 16 * half)
                    dve.tensor_scalar(x1_out[:, par], y[:, par], mean_var[:, par, 0:1], rstd[:, par:par + 1],
                                      ALU.subtract, ALU.mult).then_inc(x1_done, 1)

            steps(dve, step, LAGS, TILES, LAGS)
            dve.wait_ge(lo_seen, SLABS)
            dve.tensor_reduce(lo_top1[:, 0:1], lo_top[:, :], AX.X, ALU.max).then_inc(lo_reduced, 1)
            dve.wait_ge(lo_joined, 1)
            dve.tensor_scalar(inexact[:, :], lo_top1[:, 1:2], 0.0, None, ALU.is_gt).then_inc(flag_set, 1)
            dve.wait_ge(flag_set, 1)


def ffn_phase(nc, x1, ffn_hi, ffn_lo, inexact, scales, down_s, eye, out):
    BLOCKS = x1.shape[0] // 4
    T4 = 4
    SLABS = ffn_hi.shape[0]
    x1_blocks = x1.rearrange("(m t) p e -> m p t e", t=T4)
    out_blocks = out.rearrange("(m t) p e -> m t p e", t=T4)
    with ExitStack() as ctx:
        def sb(name, shape, dt=F32):
            return ctx.enter_context(nc.sbuf_tensor(name, shape, dt))

        def bank(name):
            return ctx.enter_context(nc.psum_tensor(name, [P, E], F32))

        def sem(name):
            return ctx.enter_context(nc.semaphore(name))

        wf_hi = sb("wf_hi", [P, NJ, CHUNK], F32R)
        wf_lo = sb("wf_lo", [P, NJ, CHUNK], F32R)
        idn = sb("idn", [P, P])
        gu_scale = sb("gu_scale", [P, 2, NJ])
        dscale = sb("dscale", [P, E])
        xr = sb("xr", [P, 2, T4, E])
        xT_hi = sb("xT_hi", [P, 2, KE, E], F32R)
        xT_lo = sb("xT_lo", [P, 2, KE, E], F32R)
        act_g = sb("act_g", [P, E])
        hid = sb("hid", [P, E])
        hid_hi = sb("hid_hi", [P, 2, E], F32R)
        hid_lo = sb("hid_lo", [P, 2, E], F32R)
        z = sb("z", [P, T4, E])
        st = sb("st", [P, T4, 6])
        mv = sb("mv", [P, T4, 2])
        rs = sb("rs", [P, T4])
        pw = sb("pw", [P, T4])

        pair_bank = [[bank(f"ps_{n}{b}") for n in "gu"] for b in range(2)]
        acc = [bank(f"acc{t}") for t in range(T4)]

        hi_loaded = [sem(f"hi_loaded{j}") for j in range(NJ)]
        lo_loaded = [sem(f"lo_loaded{j}") for j in range(NJ)]
        c_loaded, pw_set = sem("c_loaded"), sem("pw_set")
        xr_loaded = [sem(f"xr_loaded{u}") for u in range(2)]
        out_stored = sem("out_stored")
        gu_done, silu_done, hid_done, hhi_done, hlo_done, down_done = (
            sem("gu_done"), sem("silu_done"), sem("hid_done"), sem("hhi_done"), sem("hlo_done"), sem("down_done"))
        tr_done, xThi_done, xTlo_done = sem("tr_done"), sem("xThi_done"), sem("xTlo_done")
        acc_read, z_added, st_done, mv_done, rs_done, z_done = (
            sem("acc_read"), sem("z_added"), sem("st_done"), sem("mv_done"), sem("rs_done"), sem("z_done"))

        T_AT = {3: 0, 6: 1}
        order = []
        for j in range(NJ):
            order.append(("chunk", j))
            if j in T_AT:
                order.append(("turn", T_AT[j]))
        SLOTS = len(order)
        assert SLOTS % 2 == 1

        def slot(u, item):
            return pair_bank[(SLOTS * u + order.index(item)) % 2]

        def wait_slot(pe, i, u, item):
            s = order.index(item) - 2
            m = 2 * i + u
            if s < 0:
                s, m = s + SLOTS, m - 1
            kind, k = order[s]
            if kind == "turn":
                if not isinstance(m, int) or 0 <= m < BLOCKS:
                    at_least(pe, xThi_done, 4 * m + 2 * k + 2)
                    at_least(pe, xTlo_done, 4 * m + 2 * k + 2)
            elif not isinstance(m, int) or 1 <= m < BLOCKS + 1:
                at_least(pe, silu_done, NJ * (m - 1) + k + 1)
                at_least(pe, hid_done, NJ * (m - 1) + k + 1)

        LAGS = 2
        PEEL = 4
        block = ctx.enter_context(nc.Block())

        @block.sync
        def _(sp):
            sp.dma_start(idn[:, :], eye).then_inc(c_loaded, 16)
            sp.dma_start(xr[:, 0], x1_blocks[0]).then_inc(xr_loaded[0], 16)
            sp.dma_start(gu_scale[:, :, :], scales).then_inc(c_loaded, 16)
            sp.dma_start(dscale[:, :], down_s.to_broadcast([P, E])).then_inc(c_loaded, 16)
            hi_src = ffn_hi.rearrange("s p c -> p s c")
            lo_src = ffn_lo.rearrange("s p c -> p s c")
            SW = FFN // SLABS

            def load_chunk(dst, src, j, loaded):
                lo, end, parts = j * CHUNK, (j + 1) * CHUNK, 0
                while lo < end:
                    s, off = lo // SW, lo % SW
                    whole = (end - lo) // SW if off == 0 else 0
                    if whole:
                        n = whole * SW
                        sp.dma_start(dst[:, j, lo - j * CHUNK:lo - j * CHUNK + n].bitcast(F32)
                                     .rearrange("p (s c) -> p s c", c=SW), src[:, s:s + whole]).then_inc(loaded, 16)
                    else:
                        n = min(SW - off, end - lo)
                        sp.dma_start(dst[:, j, lo - j * CHUNK:lo - j * CHUNK + n].bitcast(F32),
                                     src[:, s, off:off + n]).then_inc(loaded, 16)
                    lo += n
                    parts += 1
                return parts

            for j in range(NJ):
                hi_parts[j] = load_chunk(wf_hi, hi_src, j, hi_loaded[j])
            with sp.If(sp.value_load(inexact[0:1, 0:1], min_val=0, max_val=1)):
                for j in range(NJ):
                    lo_parts[j] = load_chunk(wf_lo, lo_src, j, lo_loaded[j])

            def step(i, u):
                if t := tile_of(i, u, 0, BLOCKS):
                    m, half, par = t
                    if not (isinstance(m, int) and m == 0):
                        at_least(sp, z_added, T4 * (m - 1))
                        sp.dma_start(xr[:, par], x1_blocks[m]).then_inc(xr_loaded[par], 16)
                if t := tile_of(i, u, 2, BLOCKS):
                    m, half, par = t
                    for r in range(T4):
                        sp.wait_ge(z_done, T4 * m + r + 1)
                        sp.dma_start(out_blocks[m, r], z[:, r]).then_inc(out_stored, 16)

            steps(sp, step, PEEL, BLOCKS, LAGS)
            sp.wait_ge(out_stored, 16 * T4 * BLOCKS)

        @block.tensor
        def _(pe):
            pe.wait_ge(c_loaded, 48)
            def products(with_lo):

                def gate_up(i, u, j):
                    m, half, par = tile_of(i, u, 1, BLOCKS)
                    banks = slot(u, ("chunk", j))
                    if j == 0:
                        pe.wait_ge(xThi_done, 4 * m + 4)
                        pe.wait_ge(xTlo_done, 4 * m + 4)
                    if isinstance(m, int) and m == 0:
                        pe.wait_ge(hi_loaded[j], 16 * hi_parts[j])
                        if with_lo:
                            pe.wait_ge(lo_loaded[j], 16 * lo_parts[j])
                    wait_slot(pe, i, u, ("chunk", j))
                    for g in range(2):
                        for k in range(KE):
                            cols = slice((g * KE + k) * P, (g * KE + k + 1) * P)
                            pe.matmul(banks[g][:, :], wf_hi[:, j, cols], xT_hi[:, par, k], start=(k == 0), stop=False)
                            if with_lo:
                                pe.matmul(banks[g][:, :], wf_lo[:, j, cols], xT_hi[:, par, k], start=False, stop=False)
                            last = pe.matmul(banks[g][:, :], wf_hi[:, j, cols], xT_lo[:, par, k],
                                             start=False, stop=(k == KE - 1))
                    last.then_inc(gu_done, 1)

                def down(i, u, lag, j):
                    m, half, par = tile_of(i, u, lag, BLOCKS)
                    hp = (NJ * par + j) % 2
                    pe.wait_ge(hhi_done, NJ * m + j + 1)
                    pe.wait_ge(hlo_done, NJ * m + j + 1)
                    if j == 0:
                        at_least(pe, acc_read, T4 * m)
                    wd = slice(2 * KE * P, CHUNK)
                    for r in range(T4):
                        rows = slice(r * P, (r + 1) * P)
                        pe.matmul(acc[r][:, :], hid_hi[:, hp, rows], wf_hi[:, j, wd], start=(j == 0), stop=False)
                        if with_lo:
                            pe.matmul(acc[r][:, :], hid_hi[:, hp, rows], wf_lo[:, j, wd], start=False, stop=False)
                        last = pe.matmul(acc[r][:, :], hid_lo[:, hp, rows], wf_hi[:, j, wd],
                                         start=False, stop=(j == NJ - 1))
                    last.then_inc(down_done, 1)

                def turn(i, u, s):
                    m, half, par = tile_of(i, u, 0, BLOCKS)
                    banks = slot(u, ("turn", s))
                    pe.wait_ge(xr_loaded[par], 16 * (half + 1))
                    wait_slot(pe, i, u, ("turn", s))
                    if s == 1:
                        pe.wait_ge(xThi_done, 4 * m + 2)
                        pe.wait_ge(xTlo_done, 4 * m + 2)
                    for g in range(2):
                        k = 2 * s + g
                        for r in range(T4):
                            last = pe.transpose(banks[g][:, r * P:(r + 1) * P], xr[:, par, r, k * P:(k + 1) * P],
                                                idn[:, :])
                    last.then_inc(tr_done, 1)

                def step(i, u):
                    for j in range(NJ):
                        if tile_of(i, u, 1, BLOCKS):
                            gate_up(i, u, j)
                        if j == 0 and tile_of(i, u, 2, BLOCKS):
                            down(i, u, 2, NJ - 1)
                        if j > 0 and tile_of(i, u, 1, BLOCKS):
                            down(i, u, 1, j - 1)
                        if j in T_AT and tile_of(i, u, 0, BLOCKS):
                            turn(i, u, T_AT[j])

                steps(pe, step, PEEL, BLOCKS, LAGS)

            with pe.If(pe.value_load(inexact[0:1, 0:1], min_val=0, max_val=1)):
                products(True)
            with pe.Else():
                products(False)

        @block.scalar
        def _(act):
            act.wait_ge(c_loaded, 48)

            def hidden(i, u, j):
                m, half, par = tile_of(i, u, 1, BLOCKS)
                c = NJ * m + j
                hp = (NJ * par + j) % 2
                act.wait_ge(gu_done, c + 1)
                at_least(act, hid_done, c)
                act.activation(act_g[:, :], slot(u, ("chunk", j))[0][:, :], ACT.Silu,
                               scale=gu_scale[:, 0, j:j + 1]).then_inc(silu_done, 1)
                act.wait_ge(hid_done, c + 1)
                at_least(act, down_done, c - 1)
                act.activation(hid_hi[:, hp], hid[:, :], ACT.Copy).then_inc(hhi_done, 1)

            def step(i, u):
                for j in range(NJ):
                    if tile_of(i, u, 1, BLOCKS):
                        hidden(i, u, j)
                    if j in T_AT and tile_of(i, u, 0, BLOCKS):
                        m, half, par = tile_of(i, u, 0, BLOCKS)
                        act.wait_ge(tr_done, 2 * m + T_AT[j] + 1)
                        if T_AT[j] == 0:
                            at_least(act, gu_done, NJ * (m - 1))
                        for g in range(2):
                            act.activation(xT_hi[:, par, 2 * T_AT[j] + g], slot(u, ("turn", T_AT[j]))[g][:, :],
                                           ACT.Copy).then_inc(xThi_done, 1)

            steps(act, step, PEEL, BLOCKS, LAGS)

        @block.gpsimd
        def _(pool):
            pool.memset(pw[:, :], -0.5).then_inc(pw_set, 1)
            pool.wait_ge(pw_set, 1)

            def step(i, u):
                if t := tile_of(i, u, 2, BLOCKS):
                    m, half, par = t
                    for r in range(T4):
                        pool.wait_ge(acc_read, T4 * m + r + 1)
                        pool.tensor_tensor(z[:, r], z[:, r], xr[:, par, r], ALU.add).then_inc(z_added, 1)
                    pool.wait_ge(mv_done, m + 1)
                    pool.tensor_tensor(rs[:, :], mv[:, :, 1], pw[:, :], ALU.pow).then_inc(rs_done, 1)

            steps(pool, step, PEEL, BLOCKS, LAGS)

        @block.vector
        def _(dve):
            dve.wait_ge(c_loaded, 48)

            def hidden(i, u, j):
                m, half, par = tile_of(i, u, 1, BLOCKS)
                c = NJ * m + j
                hp = (NJ * par + j) % 2
                dve.wait_ge(silu_done, c + 1)
                at_least(dve, hhi_done, c)
                at_least(dve, hlo_done, c)
                dve.scalar_tensor_tensor(out=hid[:, :], in0=slot(u, ("chunk", j))[1][:, :],
                                         scalar=gu_scale[:, 1, j:j + 1], in1=act_g[:, :],
                                         op0=ALU.mult, op1=ALU.mult).then_inc(hid_done, 1)
                dve.wait_ge(hhi_done, c + 1)
                if j == 3:
                    at_least(dve, st_done, 8 * (m - 1) + 4)
                dve.tensor_tensor(hid_lo[:, hp], hid[:, :], hid_hi[:, hp].bitcast(F32), ALU.subtract)\
                   .then_inc(hlo_done, 1)

            def read_sums(m):
                dve.wait_ge(down_done, NJ * (m + 1))
                for r in range(T4):
                    at_least(dve, out_stored, 16 * T4 * m)
                    dve.tensor_tensor(z[:, r], acc[r][:, :], dscale[:, :], ALU.mult).then_inc(acc_read, 1)

            def stats_of(m):
                for r in range(T4):
                    dve.wait_ge(z_added, T4 * m + r + 1)
                    dve.bn_stats(st[:, r], z[:, r]).then_inc(st_done, 1)

            def moments(m):
                if isinstance(m, int):
                    dve.wait_ge(st_done, 8 * m + 4)
                for r in range(T4):
                    dve.bn_aggr(mv[:, r], st[:, r]).then_inc(st_done, 1)
                dve.wait_ge(st_done, 8 * m + 8)
                dve.tensor_scalar(mv[:, :, 1], mv[:, :, 1], EPS, None, ALU.add).then_inc(mv_done, 1)

            def normalise(m):
                dve.wait_ge(rs_done, m + 1)
                for r in range(T4):
                    dve.tensor_scalar(z[:, r], z[:, r], mv[:, r, 0:1], rs[:, r:r + 1],
                                      ALU.subtract, ALU.mult).then_inc(z_done, 1)

            def step(i, u):
                for j in range(NJ):
                    if tile_of(i, u, 1, BLOCKS):
                        hidden(i, u, j)
                    if t := tile_of(i, u, 2, BLOCKS):
                        if j == 0:
                            read_sums(t[0])
                        if j == 2:
                            stats_of(t[0])
                        if j == 3:
                            moments(t[0])
                        if j == 5:
                            normalise(t[0])
                    if j in T_AT and tile_of(i, u, 0, BLOCKS):
                        m, half, par = tile_of(i, u, 0, BLOCKS)
                        s = T_AT[j]
                        for g in range(2):
                            dve.wait_ge(xThi_done, 4 * m + 2 * s + g + 1)
                            dve.tensor_tensor(xT_lo[:, par, 2 * s + g], slot(u, ("turn", s))[g][:, :],
                                              xT_hi[:, par, 2 * s + g].bitcast(F32), ALU.subtract)\
                               .then_inc(xTlo_done, 1)

            steps(dve, step, PEEL, BLOCKS, LAGS)


hi_parts, lo_parts = {}, {}


def post_ln_layer(nc, x_cols, x_rows, rope, w_qkvo, biases, ffn_w, scales, down_s, eye, head_mask, out):
    tiles = x_cols.shape[0]
    x1 = nc.dram_tensor("x1_rows", [tiles, P, E], F32, kind="Internal").ap()
    ffn_hi = nc.dram_tensor("ffn_hi", [tiles // 2, P, 2 * FFN // tiles], F32, kind="Internal").ap()
    ffn_lo = nc.dram_tensor("ffn_lo", [tiles // 2, P, 2 * FFN // tiles], F32, kind="Internal").ap()
    with nc.sbuf_tensor("inexact", [P, 1], mybir.dt.int32) as inexact:
        attention_phase(nc, x_cols, x_rows, rope, w_qkvo, biases, ffn_w, eye, head_mask, x1, ffn_hi, ffn_lo, inexact)
        ffn_phase(nc, x1, ffn_hi, ffn_lo, inexact, scales, down_s, eye, out)




def kernel(**inputs):
    import numpy as np
    import concourse.bacc as bacc
    from concourse import mybir as mb
    from concourse.bass_utils import run_bass_kernel_spmd

    x = np.asarray(inputs["L0_attn_x"])
    NB, S, _ = x.shape
    TB = S // P
    con = np.ascontiguousarray
    by_tile = x.reshape(NB, TB, A8, B4, C, E).transpose(0, 1, 4, 3, 2, 5).reshape(NB * TB, P, E)
    by_row = x.reshape(NB, H, TB, A8, E).transpose(0, 2, 1, 3, 4).reshape(NB * TB, P, E)
    T = lambda name: np.asarray(inputs[name]).T
    square = lambda w: w.reshape(KE, P, E).transpose(1, 0, 2)
    gate = T("L0_ffn_gate_w").reshape(KE, P, NJ, P).transpose(1, 2, 0, 3).reshape(P, NJ, KE * P)
    up = T("L0_ffn_up_w").reshape(KE, P, NJ, P).transpose(1, 2, 0, 3).reshape(P, NJ, KE * P)
    down = T("L0_ffn_down_w").reshape(NJ, P, E).transpose(1, 0, 2)
    slabs = NB * TB // 2
    ffn = np.concatenate([gate, up, down], axis=2).reshape(P, slabs, FFN // slabs).transpose(1, 0, 2)
    inv = (1.0 / np.float32(10000.0) ** (np.arange(0, D, 2, dtype=np.float32) / np.float32(D))).astype(np.float32)
    angle = np.outer(np.arange(S, dtype=np.float32), inv).astype(np.float32)
    cos, sin = np.cos(angle).astype(np.float32), np.sin(angle).astype(np.float32)
    table = np.stack([np.stack([cos, cos], -1), np.stack([-sin, sin], -1)], 1).reshape(S, 2, D)
    table = table.reshape(TB, A8, B4, C, 2, D).transpose(0, 3, 2, 1, 4, 5).reshape(TB, P, 2, D)
    per_chunk = lambda name: np.asarray(inputs[name]).reshape(NJ, P).T
    arrays = {
        "x_cols": con(by_tile.reshape(NB * TB, P, KE, P).transpose(0, 3, 2, 1)),
        "x_rows": con(by_row),
        "rope": con(table),
        "w_qkvo": con(np.stack([square(T("L0_attn_W" + w)) for w in "qkvo"])),
        "biases": con(np.stack([np.asarray(inputs["L0_attn_b" + w]) for w in "qkvo"])),
        "ffn_w": con(ffn),
        "scales": con(np.stack([per_chunk("L0_ffn_gate_s"), per_chunk("L0_ffn_up_s")], 1)),
        "down_s": con(np.asarray(inputs["L0_ffn_down_s"]).reshape(1, E)),
        "eye": np.eye(P, dtype=np.float32),
        "head_mask": con(np.tile(np.eye(A8, dtype=np.float32), (H, 1))),
    }
    nc = bacc.Bacc("TRN2", target_bir_lowering=False, num_devices=1)
    args = [nc.dram_tensor(name, a.shape, mb.dt.from_np(a.dtype), kind="ExternalInput").ap()
            for name, a in arrays.items()]
    out = nc.dram_tensor("out", (NB * TB, P, E), mb.dt.float32, kind="ExternalOutput").ap()
    post_ln_layer(nc, *args, out)
    got = run_bass_kernel_spmd(nc, [arrays], core_ids=[0]).results[0]["out"]
    return con(got.reshape(NB, TB, H, A8, E).transpose(0, 2, 1, 3, 4).reshape(NB, S, E))
```

```python
from contextlib import ExitStack

import concourse.bass as bass
from concourse import mybir

ALU = mybir.AluOpType
ACT = mybir.ActivationFunctionType
AX = mybir.AxisListType
F32 = mybir.dt.float32
F32R = mybir.dt.float32r

P = 128
E = 512
H = 16
D = E // H
KE = E // P
C = 4
B4 = 4
A8 = 8
I = B4 * A8
Q32 = 32
INTER = 1408
NJ = INTER // P
CHUNK = 2 * KE * P + E
FFN = NJ * CHUNK
EPS = 1e-5
SCALE = float(D) ** -0.5


def at_least(eng, sem, count):
    if isinstance(count, int) and count <= 0:
        return
    eng.wait_ge(sem, count)


def steps(eng, step, peel, total, tail):
    for n in range(peel):
        step(n // 2, n % 2)
    with eng.Fori(peel // 2, total // 2) as i:
        for u in range(2):
            step(i, u)
    for n in range(total, total + tail):
        step(n // 2, n % 2)


def tile_of(i, u, lag, count):
    m, half, par = 2 * i + (u - lag), i + (u - lag) // 2, (u - lag) % 2
    if isinstance(m, int) and not 0 <= m < count:
        return None
    return m, half, par


class Shared:

    def __init__(self, nc, ctx):
        def sb(name, shape, dt=F32):
            return ctx.enter_context(nc.sbuf_tensor(name, shape, dt))

        def sem(name):
            return ctx.enter_context(nc.semaphore(name))

        self.inexact = sb("inexact", [P, 1], mybir.dt.int32)
        self.wide = sb("wide", [P, 2, 4, E])
        self.wf_first = sb("wf_first", [P, CHUNK], F32R)
        self.xr_loaded = [sem(f"xr_loaded{u}") for u in range(2)]
        self.cols_loaded, self.first_loaded = sem("cols_loaded"), sem("first_loaded")
        self.x1_stored = [sem(f"x1_stored{u}") for u in range(2)]
        self.x1_cols_stored = [sem(f"x1_cols_stored{u}") for u in range(2)]
        self.f_hi_stored, self.f_lo_stored = sem("f_hi_stored"), sem("f_lo_stored")


def load_chunk(eng, dst, src, j, loaded):
    slab, lo, end, parts = src.shape[2], j * CHUNK, (j + 1) * CHUNK, 0
    while lo < end:
        s, off, at = lo // slab, lo % slab, lo - j * CHUNK
        whole = (end - lo) // slab if off == 0 else 0
        n = whole * slab if whole else min(slab - off, end - lo)
        if whole:
            eng.dma_start(dst[:, at:at + n].bitcast(F32).rearrange("p (s c) -> p s c", c=slab),
                          src[s:s + whole].rearrange("s p c -> p s c")).then_inc(loaded, 16)
        else:
            eng.dma_start(dst[:, at:at + n].bitcast(F32), src[s, :, off:off + n]).then_inc(loaded, 16)
        lo += n
        parts += 1
    return parts


def attention_phase(nc, shared, x_cols, x_rows, rope, w_qkvo, biases, ffn_w, eye, head_mask, x1, x1_cols, ffn_hi,
                    ffn_lo):
    TILES = x_cols.shape[0]
    LAGS = 8
    SLABS = TILES // 2
    SLAB = FFN // SLABS
    assert SLAB * SLABS == FFN
    with ExitStack() as ctx:
        def sb(name, shape, dt=F32):
            return ctx.enter_context(nc.sbuf_tensor(name, shape, dt))

        def bank(name):
            return ctx.enter_context(nc.psum_tensor(name, [P, E], F32))

        def sem(name):
            return ctx.enter_context(nc.semaphore(name))

        w_raw = shared.wide
        w_hi = sb("w_hi", [P, 4, KE, E], F32R)
        w_lo = sb("w_lo", [P, 4, KE, E], F32R)
        bias = sb("bias", [P, 4, E])
        ident = sb("ident", [P, P])
        own_token = sb("own_token", [P, A8])
        xc = sb("xc", [P, 2, KE, P])
        xc_hi = sb("xc_hi", [P, 2, KE, P], F32R)
        xc_lo = sb("xc_lo", [P, 2, KE, P], F32R)
        rot = sb("rot", [P, 2, 2, D])
        qk_in = sb("qk_in", [P, 2, E])
        qk_cos = sb("qk_cos", [P, 2, E])
        qk_sin = sb("qk_sin", [P, 2, E])
        qk_rot = sb("qk_rot", [P, 2, E])
        v_in = sb("v_in", [P, E])
        qT = sb("qT", [P, 2, I, H])
        kT = sb("kT", [P, I, H])
        kX = sb("kX", [P, I, C, H])
        vT = sb("vT", [P, 2, B4, H, A8])
        v8 = sb("v8", [P, 2, B4, P])
        prob = sb("prob", [P, 2, A8 * C, H])
        top = sb("top", [P, A8 * C])
        total = sb("total", [P, A8 * C])
        over = sb("over", [P, A8 * C])
        probN = sb("probN", [P, C, H, A8])
        probX = sb("probX", [P, C * B4, H, A8])
        aT_hi = sb("aT_hi", [P, 2, B4, P], F32R)
        aT_lo = sb("aT_lo", [P, 2, B4, P], F32R)
        res = sb("res", [P, 2, E])
        res_bo = sb("res_bo", [P, 2, E])
        y = sb("y", [P, 2, E])
        stats = sb("stats", [P, 6])
        mean_var = sb("mean_var", [P, 2, 2])
        rstd = sb("rstd", [P, 2])
        power = sb("power", [P, 1])
        x1_out = sb("x1_out", [P, 2, E])
        x1_turn = sb("x1_turn", [P, 2, KE, KE, Q32])
        f_raw = sb("f_raw", [P, SLAB])
        f_hi = sb("f_hi", [P, SLAB], F32R)
        f_lo = sb("f_lo", [P, SLAB], F32R)
        lo_top = sb("lo_top", [P, SLABS])
        lo_top1 = sb("lo_top1", [P, 2])

        ps_qkv = [bank("ps_q"), bank("ps_k"), bank("ps_v")]
        ps_s, ps_p, ps_vt, ps_a, ps_o = bank("ps_s"), bank("ps_p"), bank("ps_vt"), bank("ps_a"), bank("ps_o")

        w_loaded = [[sem(f"w_loaded{w}_{k}") for k in range(KE)] for w in range(4)]
        w_hi_done, w_lo_done = sem("w_hi_done"), sem("w_lo_done")
        const_loaded = sem("const_loaded")
        kX_zeroed, power_set, idle_cleared = sem("kX_zeroed"), sem("power_set"), sem("idle_cleared")
        xc_loaded = [sem(f"xc_loaded{u}") for u in range(2)]
        rot_loaded = [sem(f"rot_loaded{u}") for u in range(2)]
        res_loaded = [sem(f"res_loaded{u}") for u in range(2)]
        x1_stored, x1_cols_stored = shared.x1_stored, shared.x1_cols_stored
        f_loaded, f_hi_done, f_lo_done = sem("f_loaded"), sem("f_hi_done"), sem("f_lo_done")
        f_hi_stored, f_lo_stored = shared.f_hi_stored, shared.f_lo_stored
        xhi_done, xlo_done = sem("xhi_done"), sem("xlo_done")
        proj_done = [sem(f"proj_done_{w}") for w in "qkv"]
        biased = [sem(f"biased_{w}") for w in "qkv"]
        cos_done = [sem(f"cos_done_{w}") for w in "qk"]
        sin_done = [sem(f"sin_done_{w}") for w in "qk"]
        rotated = [sem(f"rotated_{w}") for w in "qk"]
        turned = [sem(f"turned_{w}") for w in "qkv"]
        k_spread = sem("k_spread")
        scores_done, max_done, sub_done, exp_done = sem("scores_done"), sem("max_done"), sem("sub_done"), sem("exp_done")
        sum_done, over_done, prob_done = sem("sum_done"), sem("over_done"), sem("prob_done")
        probT_done, spread_done, vt_done, v8_done = sem("probT_done"), sem("spread_done"), sem("vt_done"), sem("v8_done")
        av_done, ahi_done, alo_done, o_done = sem("av_done"), sem("ahi_done"), sem("alo_done"), sem("o_done")
        res_added, y_done, stats_done, aggr_done = sem("res_added"), sem("y_done"), sem("stats_done"), sem("aggr_done")
        rstd_ready, x1_done = sem("rstd_ready"), sem("x1_done")
        x1_turned = sem("x1_turned")
        lo_seen, lo_reduced, lo_joined, flag_set = sem("lo_seen"), sem("lo_reduced"), sem("lo_joined"), sem("flag_set")

        block = ctx.enter_context(nc.Block())

        @block.sync
        def _(sp):
            for w in range(4):
                for k in range(KE):
                    if w >= 2:
                        sp.wait_ge(w_hi_done, KE * (w - 2) + k + 1)
                        sp.wait_ge(w_lo_done, KE * (w - 2) + k + 1)
                    sp.dma_start(w_raw[:, w % 2, k], w_qkvo[w, :, k]).then_inc(w_loaded[w][k], 16)
                    if w == 0 and k == 0:
                        sp.dma_start(xc[:, 0], x_cols[0]).then_inc(xc_loaded[0], 16)
                if w == 1:
                    for k in range(4):
                        sp.dma_start(bias[:, k], biases[k:k + 1, :].to_broadcast([P, E])).then_inc(const_loaded, 16)
                    sp.dma_start(ident[:, :], eye).then_inc(const_loaded, 16)
                    sp.dma_start(own_token[:, :], head_mask).then_inc(const_loaded, 16)

            def first_of_next_phase():
                for v in range(2):
                    sp.wait_ge(x1_stored[v], 16 * 2)
                    sp.wait_ge(x1_cols_stored[v], 16 * C * 2)
                sp.wait_ge(w_lo_done, 4 * KE)
                sp.dma_start(shared.wide[:, 0], x1[0:4].rearrange("t p e -> p t e")).then_inc(shared.xr_loaded[0], 16)
                sp.dma_start(shared.wide[:, 1], x1_cols[0:4].rearrange("t f e q c -> (f e) t (q c)"))\
                  .then_inc(shared.cols_loaded, 16)
                sp.wait_ge(f_hi_stored, 16 * (SLABS // 2))
                first_parts.append(load_chunk(sp, shared.wf_first, ffn_hi, 0, shared.first_loaded))

            def step(i, u):
                if isinstance(i, int) and 2 * i + u == TILES:
                    first_of_next_phase()
                if t := tile_of(i, u, 0, TILES):
                    n, half, par = t
                    if not (isinstance(n, int) and n == 0):
                        at_least(sp, xhi_done, n - 1)
                        at_least(sp, xlo_done, n - 1)
                        sp.dma_start(xc[:, par], x_cols[n]).then_inc(xc_loaded[par], 16)
                    at_least(sp, rotated[1], n - 1)
                    sp.dma_start(rot[:, par], rope[n % rope.shape[0]]).then_inc(rot_loaded[par], 16)
                if t := tile_of(i, u, 3, TILES):
                    n, half, par = t
                    at_least(sp, res_added, n - 1)
                    sp.dma_start(res[:, par], x_rows[n]).then_inc(res_loaded[par], 16)
                if u == 0 and (t := tile_of(i, u, 2, TILES)):
                    slab = t[1]
                    at_least(sp, f_hi_done, slab)
                    at_least(sp, f_lo_done, slab)
                    sp.dma_start(f_raw[:, :], ffn_w[slab]).then_inc(f_loaded, 16)
                if u == 0 and (t := tile_of(i, u, 4, TILES)):
                    slab = t[1]
                    sp.wait_ge(f_hi_done, slab + 1)
                    sp.dma_start(ffn_hi[slab], f_hi[:, :].bitcast(F32)).then_inc(f_hi_stored, 16)
                    sp.wait_ge(f_lo_done, slab + 1)
                    sp.dma_start(ffn_lo[slab], f_lo[:, :].bitcast(F32)).then_inc(f_lo_stored, 16)
                if t := tile_of(i, u, 7, TILES):
                    n, half, par = t
                    sp.wait_ge(x1_done, n + 1)
                    sp.dma_start(x1[n], x1_out[:, par]).then_inc(x1_stored[par], 16)
                    sp.wait_ge(x1_turned, n + 1)
                    for q in range(C):
                        sp.dma_start(x1_cols[n, :, :, q].rearrange("f e c -> e f c"),
                                     x1_turn[32 * q:32 * q + 32, par].rearrange("e f k r -> e f (k r)"))\
                          .then_inc(x1_cols_stored[par], 16)

            steps(sp, step, LAGS, TILES, LAGS)

        @block.tensor
        def _(pe):
            def project(out, hi, lo, w, sem_done, first_use):
                for k in range(KE):
                    if first_use:
                        pe.wait_ge(w_hi_done, KE * w + k + 1)
                        pe.wait_ge(w_lo_done, KE * w + k + 1)
                    pe.matmul(out, hi[:, k], w_hi[:, w, k], start=(k == 0), stop=False)
                    pe.matmul(out, hi[:, k], w_lo[:, w, k], start=False, stop=False)
                    last = pe.matmul(out, lo[:, k], w_hi[:, w, k], start=False, stop=(k == KE - 1))
                last.then_inc(sem_done, 1)

            def step(i, u):
                if t := tile_of(i, u, 1, TILES):
                    n, half, par = t
                    pe.wait_ge(xhi_done, n + 1)
                    pe.wait_ge(xlo_done, n + 1)
                    for w in range(3):
                        at_least(pe, biased[w], n)
                        project(ps_qkv[w][:, :], xc_hi[:, par], xc_lo[:, par], w, proj_done[w],
                                isinstance(n, int) and n == 0)
                if t := tile_of(i, u, 3, TILES):
                    n, half, par = t
                    pe.wait_ge(prob_done, n + 1)
                    at_least(pe, spread_done, n)
                    for c in range(C):
                        last = pe.transpose(ps_p[:, c * P:(c + 1) * P],
                                            probN[:, c].rearrange("p t a -> p (t a)"), ident[:, :])
                    last.then_inc(probT_done, 1)
                if t := tile_of(i, u, 2, TILES):
                    n, half, par = t
                    if isinstance(n, int) and n == 0:
                        pe.wait_ge(const_loaded, 16 * 6)
                        pe.wait_ge(idle_cleared, 1)
                    pe.wait_ge(turned[0], n + 1)
                    pe.wait_ge(k_spread, n + 1)
                    at_least(pe, sub_done, n)
                    for a in range(A8):
                        for b in range(B4):
                            last = pe.matmul(ps_s[32 * b:32 * b + H, a * C * H:(a + 1) * C * H],
                                             qT[:, par, A8 * b + a],
                                             kX[:, A8 * b + a].rearrange("p c t -> p (c t)"),
                                             start=True, stop=True, skip_group_check=True)
                    last.then_inc(scores_done, 1)
                    pe.wait_ge(turned[2], n + 1)
                    at_least(pe, v8_done, n)
                    for b in range(B4):
                        last = pe.transpose(ps_vt[:, b * P:(b + 1) * P],
                                            vT[:, par, b].rearrange("p h a -> p (h a)"), ident[:, :])
                    last.then_inc(vt_done, 1)
                if t := tile_of(i, u, 4, TILES):
                    n, half, par = t
                    pe.wait_ge(ahi_done, n + 1)
                    pe.wait_ge(alo_done, n + 1)
                    at_least(pe, y_done, n)
                    project(ps_o[:, :], aT_hi[:, par], aT_lo[:, par], 3, o_done,
                            isinstance(n, int) and n == 0)
                if t := tile_of(i, u, 3, TILES):
                    n, half, par = t
                    pe.wait_ge(spread_done, n + 1)
                    pe.wait_ge(v8_done, n + 1)
                    at_least(pe, ahi_done, n)
                    at_least(pe, alo_done, n)
                    for b in range(B4):
                        for c in range(C):
                            last = pe.matmul(ps_a[32 * c:32 * c + 32, b * P:(b + 1) * P],
                                             v8[:, par, b, 32 * c:32 * c + 32],
                                             probX[:, c * B4 + b].rearrange("p h a -> p (h a)"),
                                             start=True, stop=True, skip_group_check=True)
                    last.then_inc(av_done, 1)

            steps(pe, step, LAGS, TILES, LAGS)

        @block.scalar
        def _(act):
            def split_x(n, half, par):
                act.wait_ge(xc_loaded[par], 16 * (half + 1))
                at_least(act, proj_done[2], n - 1)
                act.activation(xc_hi[:, par], xc[:, par], ACT.Copy).then_inc(xhi_done, 1)

            for w in range(4):
                for k in range(KE):
                    act.wait_ge(w_loaded[w][k], 16)
                    act.activation(w_hi[:, w, k], w_raw[:, w % 2, k], ACT.Copy).then_inc(w_hi_done, 1)
                    if w == 0 and k == 0:
                        split_x(0, 0, 0)
            act.wait_ge(const_loaded, 16 * 6)

            def step(i, u):
                if t := tile_of(i, u, 0, TILES):
                    n, half, par = t
                    if not (isinstance(n, int) and n == 0):
                        split_x(n, half, par)
                if t := tile_of(i, u, 4, TILES):
                    n, half, par = t
                    act.wait_ge(av_done, n + 1)
                    at_least(act, o_done, n - 1)
                    act.activation(aT_hi[:, par].rearrange("p b r -> p (b r)"), ps_a[:, :], ACT.Copy)\
                        .then_inc(ahi_done, 1)
                if t := tile_of(i, u, 3, TILES):
                    n, half, par = t
                    act.wait_ge(sub_done, n + 1)
                    act.activation(prob[:, par], prob[:, par], ACT.Exp, scale=SCALE).then_inc(exp_done, 1)
                if t := tile_of(i, u, 2, TILES):
                    n, half, par = t
                    if isinstance(n, int) and n == 0:
                        act.wait_ge(kX_zeroed, 1)
                    act.wait_ge(turned[1], n + 1)
                    at_least(act, scores_done, n)
                    for c in range(C):
                        last = act.activation(kX[32 * c:32 * c + 32, :, c], kT[32 * c:32 * c + 32], ACT.Copy)
                    last.then_inc(k_spread, 1)
                if u == 0 and (t := tile_of(i, u, 2, TILES)):
                    slab = t[1]
                    act.wait_ge(f_loaded, 16 * (slab + 1))
                    at_least(act, f_hi_stored, 16 * slab)
                    at_least(act, f_lo_done, slab)
                    act.activation(f_hi[:, :], f_raw[:, :], ACT.Copy).then_inc(f_hi_done, 1)
                if t := tile_of(i, u, 3, TILES):
                    n, half, par = t
                    act.wait_ge(probT_done, n + 1)
                    at_least(act, av_done, n)
                    for a in range(A8):
                        last = act.activation(
                            probX[:, :, :, a],
                            ps_p[:, :].rearrange("p (cb used h) -> p cb used h", used=2, h=H)[:, :, 0],
                            ACT.Copy, scale=own_token[:, a:a + 1])
                    last.then_inc(spread_done, 1)
                if t := tile_of(i, u, 2, TILES):
                    n, half, par = t
                    act.wait_ge(vt_done, n + 1)
                    at_least(act, av_done, n - 1)
                    act.activation(v8[:, par].rearrange("p b r -> p (b r)"), ps_vt[:, :], ACT.Copy)\
                        .then_inc(v8_done, 1)

            steps(act, step, LAGS, TILES, LAGS)

        @block.gpsimd
        def _(pool):
            pool.wait_ge(xhi_done, 1)
            pool.tensor_tensor(xc_lo[:, 0], xc[:, 0], xc_hi[:, 0].bitcast(F32), ALU.subtract).then_inc(xlo_done, 1)
            pool.memset(kX[:, :, :, :], 0.0).then_inc(kX_zeroed, 1)
            pool.memset(power[:, :], -0.5).then_inc(power_set, 1)
            pool.wait_ge(power_set, 1)

            def step(i, u):
                if t := tile_of(i, u, 0, TILES):
                    n, half, par = t
                    if not (isinstance(n, int) and n == 0):
                        pool.wait_ge(xhi_done, n + 1)
                        pool.tensor_tensor(xc_lo[:, par], xc[:, par], xc_hi[:, par].bitcast(F32), ALU.subtract)\
                            .then_inc(xlo_done, 1)
                if t := tile_of(i, u, 4, TILES):
                    n, half, par = t
                    if isinstance(n, int) and n == 0:
                        pool.wait_ge(const_loaded, 16 * 6)
                    pool.wait_ge(res_loaded[par], 16 * (half + 1))
                    at_least(pool, y_done, n - 1)
                    pool.tensor_tensor(res_bo[:, par], res[:, par], bias[:, 3], ALU.add).then_inc(res_added, 1)
                if t := tile_of(i, u, 5, TILES):
                    n, half, par = t
                    pool.wait_ge(aggr_done, n + 1)
                    pool.tensor_tensor(rstd[:, par:par + 1], mean_var[:, par, 1:2], power[:, :], ALU.pow)\
                        .then_inc(rstd_ready, 1)
                if t := tile_of(i, u, 1, TILES):
                    n, half, par = t
                    pool.wait_ge(rot_loaded[par], 16 * (half + 1))
                    for w in range(2):
                        pool.wait_ge(biased[w], n + 1)
                        at_least(pool, rotated[w], n)
                        pool.tensor_tensor(qk_cos[:, w].rearrange("p (h d) -> p h d", h=H),
                                           qk_in[:, w].rearrange("p (h d) -> p h d", h=H),
                                           rot[:, par, 0].unsqueeze(1).to_broadcast([P, H, D]), ALU.mult)\
                            .then_inc(cos_done[w], 1)
                    pool.wait_ge(cos_done[0], n + 1)
                    pool.wait_ge(sin_done[0], n + 1)
                    at_least(pool, turned[0], n)
                    pool.tensor_tensor(qk_rot[:, 0], qk_cos[:, 0], qk_sin[:, 0], ALU.add).then_inc(rotated[0], 1)
                if u == 0 and (t := tile_of(i, u, 2, TILES)):
                    slab = t[1]
                    pool.wait_ge(f_hi_done, slab + 1)
                    at_least(pool, f_lo_stored, 16 * slab)
                    at_least(pool, lo_seen, slab)
                    pool.tensor_tensor(f_lo[:, :], f_raw[:, :], f_hi[:, :].bitcast(F32), ALU.subtract)\
                        .then_inc(f_lo_done, 1)

            steps(pool, step, LAGS, TILES, LAGS)
            pool.wait_ge(lo_reduced, 1)
            pool.partition_all_reduce(lo_top1[:, 1:2], lo_top1[:, 0:1], P, bass.bass_isa.ReduceOp.max)\
                .then_inc(lo_joined, 1)

        @block.vector
        def _(dve):
            for w in range(4):
                for k in range(KE):
                    dve.wait_ge(w_hi_done, KE * w + k + 1)
                    dve.tensor_tensor(w_lo[:, w, k], w_raw[:, w % 2, k], w_hi[:, w, k].bitcast(F32),
                                      ALU.subtract).then_inc(w_lo_done, 1)
            dve.wait_ge(const_loaded, 16 * 6)
            dve.memset(ps_s[:, :], 0.0).then_inc(idle_cleared, 1)

            def by_head(rows):
                return rows.rearrange("p (h d) -> p h d", h=H)

            def add_bias(w, n, out):
                dve.wait_ge(proj_done[w], n + 1)
                dve.tensor_tensor(out, ps_qkv[w][:, :], bias[:, w], ALU.add).then_inc(biased[w], 1)

            def sines(w, n, par):
                dve.wait_ge(biased[w], n + 1)
                dve.tensor_tensor(qk_sin[:, w].rearrange("p (h k two) -> p h k two", h=H, two=2),
                                  qk_in[:, w].rearrange("p (h k two) -> p h k two", h=H, two=2)[:, :, :, ::-1],
                                  rot[:, par, 1].rearrange("p (k two) -> p k two", two=2).unsqueeze(1)
                                  .to_broadcast([P, H, D // 2, 2]), ALU.mult).then_inc(sin_done[w], 1)

            def step(i, u):
                now1, now3, now4, now5 = (tile_of(i, u, lag, TILES) for lag in (1, 3, 4, 5))
                if now3:
                    n, half, par = now3
                    scores = ps_s[:, :].rearrange("p (g t) -> p g t", t=H)
                    dve.wait_ge(scores_done, n + 1)
                    dve.tensor_reduce(top[:, :], scores, AX.X, ALU.max).then_inc(max_done, 1)
                if now5:
                    n, half, par = now5
                    dve.wait_ge(o_done, n + 1)
                    dve.wait_ge(res_added, n + 1)
                    dve.tensor_tensor(y[:, par], ps_o[:, :], res_bo[:, par], ALU.add).then_inc(y_done, 1)
                if now3:
                    n, half, par = now3
                    dve.wait_ge(max_done, n + 1)
                    dve.tensor_tensor(prob[:, par], scores, top[:, :].unsqueeze(2).to_broadcast([P, A8 * C, H]),
                                      ALU.subtract).then_inc(sub_done, 1)
                if now5:
                    n, half, par = now5
                    dve.wait_ge(y_done, n + 1)
                    dve.bn_stats(stats[:, :], y[:, par]).then_inc(stats_done, 1)
                if now4:
                    n, half, par = now4
                    dve.wait_ge(ahi_done, n + 1)
                    at_least(dve, stats_done, 2 * (n - 1) + 1)
                    dve.tensor_tensor(aT_lo[:, par].rearrange("p b r -> p (b r)"), ps_a[:, :],
                                      aT_hi[:, par].rearrange("p b r -> p (b r)").bitcast(F32), ALU.subtract)\
                       .then_inc(alo_done, 1)
                if now5:
                    n, half, par = now5
                    if isinstance(n, int):
                        dve.wait_ge(stats_done, 2 * n + 1)
                    dve.bn_aggr(mean_var[:, par], stats[:, :]).then_inc(stats_done, 1)
                if now3:
                    n, half, par = now3
                    dve.wait_ge(exp_done, n + 1)
                    dve.tensor_reduce(total[:, :], prob[:, par], AX.X, ALU.add).then_inc(sum_done, 1)
                if now5:
                    n, half, par = now5
                    dve.wait_ge(stats_done, 2 * n + 2)
                    dve.tensor_scalar(mean_var[:, par, 1:2], mean_var[:, par, 1:2], EPS, None, ALU.add)\
                       .then_inc(aggr_done, 1)
                if now1:
                    n, half, par = now1
                    at_least(dve, rotated[0], n)
                    at_least(dve, cos_done[0], n)
                    add_bias(0, n, qk_in[:, 0])
                if now3:
                    n, half, par = now3
                    dve.wait_ge(sum_done, n + 1)
                    dve.reciprocal(over[:, :], total[:, :]).then_inc(over_done, 1)
                if now1:
                    n, half, par = now1
                    dve.wait_ge(rot_loaded[par], 16 * (half + 1))
                    sines(0, n, par)
                if now3:
                    n, half, par = now3
                    dve.wait_ge(over_done, n + 1)
                    at_least(dve, probT_done, n)
                    dve.tensor_tensor(probN[:, :].rearrange("p c t a -> p a c t"),
                                      prob[:, par].rearrange("p (a c) t -> p a c t", a=A8),
                                      over[:, :].rearrange("p (a c) -> p a c", a=A8).unsqueeze(3)
                                      .to_broadcast([P, A8, C, H]), ALU.mult).then_inc(prob_done, 1)
                if now1:
                    n, half, par = now1
                    at_least(dve, rotated[1], n)
                    at_least(dve, cos_done[1], n)
                    add_bias(1, n, qk_in[:, 1])
                if now5:
                    n, half, par = now5
                    dve.wait_ge(rstd_ready, n + 1)
                    at_least(dve, x1_stored[par], 16 * half)
                    dve.tensor_scalar(x1_out[:, par], y[:, par], mean_var[:, par, 0:1], rstd[:, par:par + 1],
                                      ALU.subtract, ALU.mult).then_inc(x1_done, 1)
                if now1:
                    n, half, par = now1
                    sines(1, n, par)
                if now5:
                    n, half, par = now5
                    dve.wait_ge(x1_done, n + 1)
                    at_least(dve, x1_cols_stored[par], 16 * C * half)
                    dve.transpose(x1_turn[:, par].rearrange("p f k r -> p k f r"),
                                  x1_out[:, par].rearrange("p (k f e) -> p k f e", k=KE, f=KE))\
                       .then_inc(x1_turned, 1)
                if now1:
                    n, half, par = now1
                    at_least(dve, turned[2], n)
                    add_bias(2, n, v_in[:, :])
                    at_least(dve, scores_done, n - 1)
                    dve.wait_ge(rotated[0], n + 1)
                    dve.transpose(qT[:, par].rearrange("p i h -> p h i"), by_head(qk_rot[:, 0])).then_inc(turned[0], 1)
                    dve.wait_ge(cos_done[1], n + 1)
                    dve.wait_ge(sin_done[1], n + 1)
                    at_least(dve, turned[1], n)
                    dve.tensor_tensor(qk_rot[:, 1], qk_cos[:, 1], qk_sin[:, 1], ALU.add).then_inc(rotated[1], 1)
                    at_least(dve, vt_done, n - 1)
                    dve.wait_ge(biased[2], n + 1)
                    dve.transpose(vT[:, par].rearrange("p b h a -> p h b a"),
                                  v_in[:, :].rearrange("p (h b a) -> p h b a", h=H, b=B4)).then_inc(turned[2], 1)
                    dve.wait_ge(rotated[1], n + 1)
                    at_least(dve, k_spread, n)
                    dve.transpose(kT[:, :].rearrange("p i h -> p h i"), by_head(qk_rot[:, 1])).then_inc(turned[1], 1)
                if u == 0 and (t := tile_of(i, u, 2, TILES)):
                    slab = t[1]
                    dve.wait_ge(f_lo_done, slab + 1)
                    dve.tensor_reduce(lo_top[:, bass.ds(slab, 1)], f_lo[:, :].bitcast(F32), AX.X, ALU.max,
                                      apply_absolute_value=True).then_inc(lo_seen, 1)

            steps(dve, step, LAGS, TILES, LAGS)
            dve.wait_ge(lo_seen, SLABS)
            dve.tensor_reduce(lo_top1[:, 0:1], lo_top[:, :], AX.X, ALU.max).then_inc(lo_reduced, 1)
            dve.wait_ge(lo_joined, 1)
            dve.tensor_scalar(shared.inexact[:, :], lo_top1[:, 1:2], 0.0, None, ALU.is_gt).then_inc(flag_set, 1)
            dve.wait_ge(flag_set, 1)


def ffn_phase(nc, shared, x1, x1_cols, ffn_hi, ffn_lo, scales, down_s, out):
    inexact = shared.inexact
    TILES = x1.shape[0]
    BLOCKS = x1.shape[0] // 4
    T4 = 4
    SLABS = ffn_hi.shape[0]
    x1_cols_blocks = x1_cols.rearrange("(m t) f e q c -> m t (f e) (q c)", t=T4)
    x1_blocks = x1.rearrange("(m t) p e -> m p t e", t=T4)
    out_blocks = out.rearrange("(m t) p e -> m t p e", t=T4)
    with ExitStack() as ctx:
        def sb(name, shape, dt=F32):
            return ctx.enter_context(nc.sbuf_tensor(name, shape, dt))

        def bank(name):
            return ctx.enter_context(nc.psum_tensor(name, [P, E], F32))

        def sem(name):
            return ctx.enter_context(nc.semaphore(name))

        wf_rest = sb("wf_rest", [P, NJ - 1, CHUNK], F32R)
        wf_lo_all = sb("wf_lo", [P, NJ, CHUNK], F32R)
        wf_hi = [shared.wf_first] + [wf_rest[:, j] for j in range(NJ - 1)]
        wf_lo = [wf_lo_all[:, j] for j in range(NJ)]
        gu_scale = sb("gu_scale", [P, 2, NJ])
        dscale = sb("dscale", [P, E])
        xr = shared.wide
        xt_raw = sb("xt_raw", [P, 2, C, KE, Q32])
        xT_hi = sb("xT_hi", [P, 2, T4, C, KE, Q32], F32R)
        xT_lo = sb("xT_lo", [P, 2, T4, C, KE, Q32], F32R)
        act_g = sb("act_g", [P, E])
        hid = sb("hid", [P, E])
        hid_hi = sb("hid_hi", [P, 2, E], F32R)
        hid_lo = sb("hid_lo", [P, 2, E], F32R)
        z = sb("z", [P, T4, E])
        st = sb("st", [P, T4, 6])
        mv = sb("mv", [P, T4, 2])
        rs = sb("rs", [P, T4])
        pw = sb("pw", [P, T4])

        pair_bank = [[bank(f"ps_{n}{b}") for n in "gu"] for b in range(2)]
        acc = [bank(f"acc{t}") for t in range(T4)]

        hi_loaded = [sem(f"hi_loaded{j}") for j in range(NJ)]
        lo_loaded = [sem(f"lo_loaded{j}") for j in range(NJ)]
        c_loaded, pw_set = sem("c_loaded"), sem("pw_set")
        xr_loaded = shared.xr_loaded
        out_stored = sem("out_stored")
        gu_done, silu_done, hid_done, hhi_done, hlo_done, down_done = (
            sem("gu_done"), sem("silu_done"), sem("hid_done"), sem("hhi_done"), sem("hlo_done"), sem("down_done"))
        xThi_done, xTlo_done = sem("xThi_done"), sem("xTlo_done")
        xt_loaded = [sem(f"xt_loaded{u}") for u in range(2)]
        acc_read, z_added, st_done, mv_done, rs_done, z_done = (
            sem("acc_read"), sem("z_added"), sem("st_done"), sem("mv_done"), sem("rs_done"), sem("z_done"))

        SPLIT_AT = {6: 0, 7: 1, 8: 2, 9: 3}

        def columns(m, t):
            if isinstance(m, int) and m == 0:
                return xr[:, 1, t].rearrange("p (q k r) -> p q k r", q=C, k=KE)
            return xt_raw[:, t % 2]

        def slot(u, j):
            return pair_bank[(NJ * u + j) % 2]

        LAGS = 2
        PEEL = 4
        block = ctx.enter_context(nc.Block())

        @block.sync
        def _(sp):
            sp.dma_start(gu_scale[:, :, :], scales).then_inc(c_loaded, 16)
            sp.dma_start(dscale[:, :], down_s.to_broadcast([P, E])).then_inc(c_loaded, 16)

            def load_columns(m, half, t):
                if not (isinstance(m, int) and T4 * m + t < T4 + 2):
                    at_least(sp, xThi_done, T4 * m + t - 1)
                    at_least(sp, xTlo_done, T4 * m + t - 1)
                sp.dma_start(xt_raw[:, t % 2].rearrange("p q k r -> p (q k r)"), x1_cols_blocks[m, t])\
                  .then_inc(xt_loaded[t % 2], 16)

            sp.wait_ge(shared.f_hi_stored, 16 * SLABS)
            sp.wait_ge(shared.f_lo_stored, 16 * SLABS)
            for j in range(1, NJ):
                hi_parts[j] = load_chunk(sp, wf_hi[j], ffn_hi, j, hi_loaded[j])
            with sp.If(sp.value_load(inexact[0:1, 0:1], min_val=0, max_val=1)):
                for j in range(NJ):
                    lo_parts[j] = load_chunk(sp, wf_lo[j], ffn_lo, j, lo_loaded[j])
            for v in range(2):
                sp.wait_ge(shared.x1_stored[v], 16 * (TILES // 2))
                sp.wait_ge(shared.x1_cols_stored[v], 16 * C * (TILES // 2))

            def step(i, u):
                if t := tile_of(i, u, 0, BLOCKS):
                    m, half, par = t
                    if isinstance(m, int) and m == 1:
                        sp.wait_ge(xThi_done, T4)
                        sp.wait_ge(xTlo_done, T4)
                    if not (isinstance(m, int) and m == 0):
                        at_least(sp, z_added, T4 * (m - 1))
                        sp.dma_start(xr[:, par], x1_blocks[m]).then_inc(xr_loaded[par], 16)
                        for t in range(T4):
                            load_columns(m, half, t)
                if t := tile_of(i, u, 2, BLOCKS):
                    m, half, par = t
                    for r in range(T4):
                        sp.wait_ge(z_done, T4 * m + r + 1)
                        sp.dma_start(out_blocks[m, r], z[:, r]).then_inc(out_stored, 16)

            steps(sp, step, PEEL, BLOCKS, LAGS)
            sp.wait_ge(out_stored, 16 * T4 * BLOCKS)

        @block.tensor
        def _(pe):
            def products(with_lo):

                def gate_up(i, u, j):
                    m, half, par = tile_of(i, u, 1, BLOCKS)
                    banks = slot(u, j)
                    if j == 0:
                        pe.wait_ge(xThi_done, T4 * m + T4)
                        pe.wait_ge(xTlo_done, T4 * m + T4)
                    if isinstance(m, int) and m == 0:
                        if j == 0:
                            pe.wait_ge(shared.first_loaded, 16 * first_parts[-1])
                        else:
                            pe.wait_ge(hi_loaded[j], 16 * hi_parts[j])
                        if with_lo:
                            pe.wait_ge(lo_loaded[j], 16 * lo_parts[j])
                    at_least(pe, silu_done, NJ * m + j - 1)
                    at_least(pe, hid_done, NJ * m + j - 1)
                    for g in range(2):
                        for k in range(KE):
                            cols = slice((g * KE + k) * P, (g * KE + k + 1) * P)
                            x_hi, x_lo = (x[:, par].rearrange("p t q k r -> p k (t q) r")[:, k]
                                          for x in (xT_hi, xT_lo))
                            pe.matmul(banks[g][:, :], wf_hi[j][:, cols], x_hi, start=(k == 0), stop=False)
                            if with_lo:
                                pe.matmul(banks[g][:, :], wf_lo[j][:, cols], x_hi, start=False, stop=False)
                            last = pe.matmul(banks[g][:, :], wf_hi[j][:, cols], x_lo,
                                             start=False, stop=(k == KE - 1))
                    last.then_inc(gu_done, 1)

                def down(i, u, lag, j):
                    m, half, par = tile_of(i, u, lag, BLOCKS)
                    hp = (NJ * par + j) % 2
                    pe.wait_ge(hhi_done, NJ * m + j + 1)
                    pe.wait_ge(hlo_done, NJ * m + j + 1)
                    wd = slice(2 * KE * P, CHUNK)
                    for r in range(T4):
                        rows = slice(r * P, (r + 1) * P)
                        if j == 0:
                            at_least(pe, acc_read, T4 * (m - 1) + r + 1)
                        pe.matmul(acc[r][:, :], hid_hi[:, hp, rows], wf_hi[j][:, wd], start=(j == 0), stop=False)
                        if with_lo:
                            pe.matmul(acc[r][:, :], hid_hi[:, hp, rows], wf_lo[j][:, wd], start=False, stop=False)
                        last = pe.matmul(acc[r][:, :], hid_lo[:, hp, rows], wf_hi[j][:, wd],
                                         start=False, stop=(j == NJ - 1))
                    last.then_inc(down_done, 1)

                def step(i, u):
                    for j in range(NJ):
                        if tile_of(i, u, 1, BLOCKS):
                            gate_up(i, u, j)
                        if j == 0 and tile_of(i, u, 2, BLOCKS):
                            down(i, u, 2, NJ - 1)
                        if j > 0 and tile_of(i, u, 1, BLOCKS):
                            down(i, u, 1, j - 1)

                steps(pe, step, PEEL, BLOCKS, LAGS)

            with pe.If(pe.value_load(inexact[0:1, 0:1], min_val=0, max_val=1)):
                products(True)
            with pe.Else():
                products(False)

        @block.scalar
        def _(act):
            act.wait_ge(c_loaded, 32)

            def hidden(i, u, j):
                m, half, par = tile_of(i, u, 1, BLOCKS)
                c = NJ * m + j
                hp = (NJ * par + j) % 2
                act.wait_ge(gu_done, c + 1)
                at_least(act, hid_done, c)
                act.activation(act_g[:, :], slot(u, j)[0][:, :], ACT.Silu,
                               scale=gu_scale[:, 0, j:j + 1]).then_inc(silu_done, 1)
                act.wait_ge(hid_done, c + 1)
                at_least(act, down_done, c - 1)
                act.activation(hid_hi[:, hp], hid[:, :], ACT.Copy).then_inc(hhi_done, 1)

            def step(i, u):
                for j in range(NJ):
                    if tile_of(i, u, 1, BLOCKS):
                        hidden(i, u, j)
                    if j in SPLIT_AT and tile_of(i, u, 0, BLOCKS):
                        m, half, par = tile_of(i, u, 0, BLOCKS)
                        t = SPLIT_AT[j]
                        if isinstance(m, int) and m == 0:
                            act.wait_ge(shared.cols_loaded, 16)
                        else:
                            act.wait_ge(xt_loaded[t % 2], 16 * (2 * (m - 1) + t // 2 + 1))
                        at_least(act, gu_done, NJ * (m - 1))
                        act.activation(xT_hi[:, par, t], columns(m, t), ACT.Copy).then_inc(xThi_done, 1)

            steps(act, step, PEEL, BLOCKS, LAGS)

        @block.gpsimd
        def _(pool):
            pool.memset(pw[:, :], -0.5).then_inc(pw_set, 1)
            pool.wait_ge(pw_set, 1)

            def step(i, u):
                if t := tile_of(i, u, 2, BLOCKS):
                    m, half, par = t
                    for r in range(T4):
                        pool.wait_ge(acc_read, T4 * m + r + 1)
                        pool.wait_ge(xr_loaded[par], 16 * (half + 1))
                        pool.tensor_tensor(z[:, r], z[:, r], xr[:, par, r], ALU.add).then_inc(z_added, 1)
                    pool.wait_ge(mv_done, m + 1)
                    pool.tensor_tensor(rs[:, :], mv[:, :, 1], pw[:, :], ALU.pow).then_inc(rs_done, 1)

            steps(pool, step, PEEL, BLOCKS, LAGS)

        @block.vector
        def _(dve):
            dve.wait_ge(c_loaded, 32)

            def hidden(i, u, j):
                m, half, par = tile_of(i, u, 1, BLOCKS)
                c = NJ * m + j
                hp = (NJ * par + j) % 2
                dve.wait_ge(silu_done, c + 1)
                at_least(dve, hhi_done, c)
                at_least(dve, hlo_done, c)
                dve.scalar_tensor_tensor(out=hid[:, :], in0=slot(u, j)[1][:, :],
                                         scalar=gu_scale[:, 1, j:j + 1], in1=act_g[:, :],
                                         op0=ALU.mult, op1=ALU.mult).then_inc(hid_done, 1)
                dve.wait_ge(hhi_done, c + 1)
                if j == 3:
                    at_least(dve, st_done, 8 * (m - 1) + 4)
                dve.tensor_tensor(hid_lo[:, hp], hid[:, :], hid_hi[:, hp].bitcast(F32), ALU.subtract)\
                   .then_inc(hlo_done, 1)

            def read_sums(m):
                dve.wait_ge(down_done, NJ * (m + 1))
                for r in range(T4):
                    at_least(dve, out_stored, 16 * T4 * m)
                    dve.tensor_tensor(z[:, r], acc[r][:, :], dscale[:, :], ALU.mult).then_inc(acc_read, 1)

            def stats_of(m):
                for r in range(T4):
                    dve.wait_ge(z_added, T4 * m + r + 1)
                    dve.bn_stats(st[:, r], z[:, r]).then_inc(st_done, 1)

            def moments(m):
                if isinstance(m, int):
                    dve.wait_ge(st_done, 8 * m + 4)
                for r in range(T4):
                    dve.bn_aggr(mv[:, r], st[:, r]).then_inc(st_done, 1)
                dve.wait_ge(st_done, 8 * m + 8)
                dve.tensor_scalar(mv[:, :, 1], mv[:, :, 1], EPS, None, ALU.add).then_inc(mv_done, 1)

            def normalise(m):
                dve.wait_ge(rs_done, m + 1)
                for r in range(T4):
                    dve.tensor_scalar(z[:, r], z[:, r], mv[:, r, 0:1], rs[:, r:r + 1],
                                      ALU.subtract, ALU.mult).then_inc(z_done, 1)

            def step(i, u):
                for j in range(NJ):
                    if tile_of(i, u, 1, BLOCKS):
                        hidden(i, u, j)
                    if t := tile_of(i, u, 2, BLOCKS):
                        if j == 0:
                            read_sums(t[0])
                        if j == 2:
                            stats_of(t[0])
                        if j == 3:
                            moments(t[0])
                        if j == 5:
                            normalise(t[0])
                    if j in SPLIT_AT and tile_of(i, u, 0, BLOCKS):
                        m, half, par = tile_of(i, u, 0, BLOCKS)
                        t = SPLIT_AT[j]
                        dve.wait_ge(xThi_done, T4 * m + t + 1)
                        dve.tensor_tensor(xT_lo[:, par, t], columns(m, t), xT_hi[:, par, t].bitcast(F32),
                                          ALU.subtract).then_inc(xTlo_done, 1)

            steps(dve, step, PEEL, BLOCKS, LAGS)


hi_parts, lo_parts, first_parts = {}, {}, []


def post_ln_layer(nc, x_cols, x_rows, rope, w_qkvo, biases, ffn_w, scales, down_s, eye, head_mask, out):
    tiles = x_cols.shape[0]
    x1 = nc.dram_tensor("x1_rows", [tiles, P, E], F32, kind="Internal").ap()
    x1_cols = nc.dram_tensor("x1_cols", [tiles, KE, Q32, C, KE * Q32], F32, kind="Internal").ap()
    ffn_hi = nc.dram_tensor("ffn_hi", [tiles // 2, P, 2 * FFN // tiles], F32, kind="Internal").ap()
    ffn_lo = nc.dram_tensor("ffn_lo", [tiles // 2, P, 2 * FFN // tiles], F32, kind="Internal").ap()
    with ExitStack() as ctx:
        shared = Shared(nc, ctx)
        attention_phase(nc, shared, x_cols, x_rows, rope, w_qkvo, biases, ffn_w, eye, head_mask, x1, x1_cols,
                        ffn_hi, ffn_lo)
        ffn_phase(nc, shared, x1, x1_cols, ffn_hi, ffn_lo, scales, down_s, out)




def kernel(**inputs):
    import numpy as np
    import concourse.bacc as bacc
    from concourse import mybir as mb
    from concourse.bass_utils import run_bass_kernel_spmd

    x = np.asarray(inputs["L0_attn_x"])
    NB, S, _ = x.shape
    TB = S // P
    con = np.ascontiguousarray
    by_tile = x.reshape(NB, TB, A8, B4, C, E).transpose(0, 1, 4, 3, 2, 5).reshape(NB * TB, P, E)
    by_row = x.reshape(NB, H, TB, A8, E).transpose(0, 2, 1, 3, 4).reshape(NB * TB, P, E)
    T = lambda name: np.asarray(inputs[name]).T
    square = lambda w: w.reshape(KE, P, E).transpose(1, 0, 2)
    gate = T("L0_ffn_gate_w").reshape(KE, P, NJ, P).transpose(1, 2, 0, 3).reshape(P, NJ, KE * P)
    up = T("L0_ffn_up_w").reshape(KE, P, NJ, P).transpose(1, 2, 0, 3).reshape(P, NJ, KE * P)
    down = T("L0_ffn_down_w").reshape(NJ, P, E).transpose(1, 0, 2)
    slabs = NB * TB // 2
    ffn = np.concatenate([gate, up, down], axis=2).reshape(P, slabs, FFN // slabs).transpose(1, 0, 2)
    inv = (1.0 / np.float32(10000.0) ** (np.arange(0, D, 2, dtype=np.float32) / np.float32(D))).astype(np.float32)
    angle = np.outer(np.arange(S, dtype=np.float32), inv).astype(np.float32)
    cos, sin = np.cos(angle).astype(np.float32), np.sin(angle).astype(np.float32)
    table = np.stack([np.stack([cos, cos], -1), np.stack([-sin, sin], -1)], 1).reshape(S, 2, D)
    table = table.reshape(TB, A8, B4, C, 2, D).transpose(0, 3, 2, 1, 4, 5).reshape(TB, P, 2, D)
    per_chunk = lambda name: np.asarray(inputs[name]).reshape(NJ, P).T
    arrays = {
        "x_cols": con(by_tile.reshape(NB * TB, P, KE, P).transpose(0, 3, 2, 1)),
        "x_rows": con(by_row),
        "rope": con(table),
        "w_qkvo": con(np.stack([square(T("L0_attn_W" + w)) for w in "qkvo"])),
        "biases": con(np.stack([np.asarray(inputs["L0_attn_b" + w]) for w in "qkvo"])),
        "ffn_w": con(ffn),
        "scales": con(np.stack([per_chunk("L0_ffn_gate_s"), per_chunk("L0_ffn_up_s")], 1)),
        "down_s": con(np.asarray(inputs["L0_ffn_down_s"]).reshape(1, E)),
        "eye": np.eye(P, dtype=np.float32),
        "head_mask": con(np.tile(np.eye(A8, dtype=np.float32), (H, 1))),
    }
    nc = bacc.Bacc("TRN2", target_bir_lowering=False, num_devices=1)
    args = [nc.dram_tensor(name, a.shape, mb.dt.from_np(a.dtype), kind="ExternalInput").ap()
            for name, a in arrays.items()]
    out = nc.dram_tensor("out", (NB * TB, P, E), mb.dt.float32, kind="ExternalOutput").ap()
    post_ln_layer(nc, *args, out)
    got = run_bass_kernel_spmd(nc, [arrays], core_ids=[0]).results[0]["out"]
    return con(got.reshape(NB, TB, H, A8, E).transpose(0, 2, 1, 3, 4).reshape(NB, S, E))
```
